# Optimizing a Trainium2 kernel written in Bass

```python
import numpy as np
import jax
import jax.numpy as jnp

def _softmax(x, axis=-1):
    return jax.nn.softmax(x, axis=axis)

def _gelu(x):
    return jax.nn.gelu(x, approximate=True)

def _silu(x):
    return jax.nn.silu(x)

def _sigmoid(x):
    return jax.nn.sigmoid(x)

def _layernorm(x, axis=-1, eps=1e-05):
    m = jnp.mean(x, axis=axis, keepdims=True)
    v = jnp.var(x, axis=axis, keepdims=True)
    return (x - m) / jnp.sqrt(v + eps)

def _scatter_add(tgt, idx, src, axis=0):
    return tgt.at[idx].add(src)

def _segment_sum(src, seg, n):
    return jax.ops.segment_sum(src, seg, n)
kernel_name = 'mk_adj_preln_d1_adj_r2_5029d9'

def setup_inputs(seed: int=0):
    np.random.seed(seed)
    _w = jnp.asarray

    def _rec_inputs():
        import jax
        import jax.numpy as jnp
        _gk = jax.random.key(seed)
        x = -0.0005207 + 1.001 * jax.random.normal(jax.random.fold_in(_gk, 1), (2048, 256), jnp.float32)
        _w = (1.0 + jnp.arange(2048, dtype=jnp.float32)) ** (-0.5)
        _w = _w / _w.mean()
        _pij = jnp.clip(0.00390625 * _w[:, None] * _w[None, :], 0.0, 1.0)
        _a = jax.random.uniform(jax.random.fold_in(_gk, 2), (2048, 2048)) < _pij
        adj = _a.astype(jnp.int32)
        _nm = jnp.ones((2048,), dtype=bool)
        nodemask = jnp.where(_nm, 1.0, 0.0).astype(jnp.int32)
        return (x, adj, nodemask)
    x, adj, nodemask = _rec_inputs()

    def _L0_gnn_setup():
        import jax, jax.numpy as jnp
        import numpy as np
        D = 256
        H = 8
        HD = D // H
        EPS = 1e-05
        NEG = -1e+30

        def layer_norm(x, scale, bias):
            mu = jnp.mean(x, axis=-1, keepdims=True)
            var = jnp.mean(jnp.square(x - mu), axis=-1, keepdims=True)
            return (x - mu) * jax.lax.rsqrt(var + EPS) * scale + bias
        key = jax.random.key(seed)
        ks = jax.random.split(key, 16)
        S = T = 2048
        inp = {'h_source': jax.random.normal(ks[0], (S, D), jnp.float32), 'h_target': jax.random.normal(ks[1], (T, D), jnp.float32), 'edge_mask': jax.random.randint(ks[2], (T, S), 0, 2, jnp.int32), 'source_mask': jnp.ones((S,), jnp.int32), 'target_mask': jnp.ones((T,), jnp.int32), 'ln1_scale': jnp.ones((D,), jnp.float32), 'ln1_bias': jnp.zeros((D,), jnp.float32), 'Wq': jax.random.normal(ks[3], (D, D), jnp.float32) / np.sqrt(D), 'bq': jnp.zeros((D,), jnp.float32), 'Wk': jax.random.normal(ks[4], (D, D), jnp.float32) / np.sqrt(D), 'bk': jnp.zeros((D,), jnp.float32), 'Wv': jax.random.normal(ks[5], (D, D), jnp.float32) / np.sqrt(D), 'bv': jnp.zeros((D,), jnp.float32), 'Wo': jax.random.normal(ks[6], (D, D), jnp.float32) / np.sqrt(D), 'bo': jnp.zeros((D,), jnp.float32), 'ln2_scale': jnp.ones((D,), jnp.float32), 'ln2_bias': jnp.zeros((D,), jnp.float32), 'W1': jax.random.normal(ks[7], (D, 4 * D), jnp.float32) / np.sqrt(D), 'W2': jax.random.normal(ks[8], (4 * D, D), jnp.float32) / np.sqrt(4 * D)}
        return inp
    _L0_gnn_all = _L0_gnn_setup()
    _L0_gnn_in = {k: v for k, v in _L0_gnn_all.items() if k in ('h_target', 'ln1_scale', 'ln1_bias', 'Wq', 'bq', 'Wk', 'bk', 'Wv', 'bv', 'Wo', 'bo', 'ln2_scale', 'ln2_bias', 'W1', 'W2')}
    del _L0_gnn_all
    return {'x': x, 'adj': adj, 'nodemask': nodemask, 'L0_gnn_h_target': _L0_gnn_in['h_target'], 'L0_gnn_ln1_scale': _L0_gnn_in['ln1_scale'], 'L0_gnn_ln1_bias': _L0_gnn_in['ln1_bias'], 'L0_gnn_Wq': _L0_gnn_in['Wq'], 'L0_gnn_bq': _L0_gnn_in['bq'], 'L0_gnn_Wk': _L0_gnn_in['Wk'], 'L0_gnn_bk': _L0_gnn_in['bk'], 'L0_gnn_Wv': _L0_gnn_in['Wv'], 'L0_gnn_bv': _L0_gnn_in['bv'], 'L0_gnn_Wo': _L0_gnn_in['Wo'], 'L0_gnn_bo': _L0_gnn_in['bo'], 'L0_gnn_ln2_scale': _L0_gnn_in['ln2_scale'], 'L0_gnn_ln2_bias': _L0_gnn_in['ln2_bias'], 'L0_gnn_W1': _L0_gnn_in['W1'], 'L0_gnn_W2': _L0_gnn_in['W2']}

def reference(x, adj, nodemask, L0_gnn_h_target, L0_gnn_ln1_scale, L0_gnn_ln1_bias, L0_gnn_Wq, L0_gnn_bq, L0_gnn_Wk, L0_gnn_bk, L0_gnn_Wv, L0_gnn_bv, L0_gnn_Wo, L0_gnn_bo, L0_gnn_ln2_scale, L0_gnn_ln2_bias, L0_gnn_W1, L0_gnn_W2):
    import jax
    import jax.numpy as jnp

    def _L0_gnn_ref(h_source, h_target, edge_mask, source_mask, target_mask, ln1_scale, ln1_bias, Wq, bq, Wk, bk, Wv, bv, Wo, bo, ln2_scale, ln2_bias, W1, W2):
        import jax, jax.numpy as jnp
        import numpy as np
        D = 256
        H = 8
        HD = D // H
        EPS = 1e-05
        NEG = -1e+30

        def layer_norm(x, scale, bias):
            mu = jnp.mean(x, axis=-1, keepdims=True)
            var = jnp.mean(jnp.square(x - mu), axis=-1, keepdims=True)
            return (x - mu) * jax.lax.rsqrt(var + EPS) * scale + bias
        smask = (source_mask == 1)[:, None]
        tmask = (target_mask == 1)[:, None]
        hs = layer_norm(h_source, ln1_scale, ln1_bias)
        ht = layer_norm(h_target, ln1_scale, ln1_bias)
        hs = jnp.where(smask, hs, 0.0)
        ht = jnp.where(tmask, ht, 0.0)
        T, S = (ht.shape[0], hs.shape[0])
        q = (ht @ Wq + bq).reshape(T, H, HD) / jnp.sqrt(jnp.float32(HD))
        k = (hs @ Wk + bk).reshape(S, H, HD)
        v = (hs @ Wv + bv).reshape(S, H, HD)
        logits = jnp.einsum('thd,shd->hts', q, k)
        logits = jnp.where(edge_mask[None] != 0, logits, NEG)
        probs = jax.nn.softmax(logits, axis=-1)
        ctx = jnp.einsum('hts,shd->thd', probs, v).reshape(T, D)
        attn = ctx @ Wo + bo
        attn = jnp.where(tmask, attn, 0.0)
        ht = ht + attn
        ht = layer_norm(ht, ln2_scale, ln2_bias)
        ht = jnp.where(tmask, ht, 0.0)
        ff = jax.nn.gelu(ht @ W1) @ W2
        return ht + ff
    h = jnp.maximum(_layernorm(x, axis=-1), 0.0)
    x = x + _L0_gnn_ref(h, L0_gnn_h_target, adj, nodemask, nodemask, L0_gnn_ln1_scale, L0_gnn_ln1_bias, L0_gnn_Wq, L0_gnn_bq, L0_gnn_Wk, L0_gnn_bk, L0_gnn_Wv, L0_gnn_bv, L0_gnn_Wo, L0_gnn_bo, L0_gnn_ln2_scale, L0_gnn_ln2_bias, L0_gnn_W1, L0_gnn_W2)
    return x

_drawn_inputs = setup_inputs


def setup_inputs(seed=0):
    import zlib

    import numpy as np

    out = dict(_drawn_inputs(seed))
    spreads = {'L0_gnn_ln1_scale': (1.0, 0.2),
     'L0_gnn_ln1_bias': (0.0, 0.1),
     'L0_gnn_bq': (0.0, 0.415),
     'L0_gnn_bk': (0.0, 0.8),
     'L0_gnn_bv': (0.0, 0.1),
     'L0_gnn_bo': (0.0, 0.1),
     'L0_gnn_ln2_scale': (1.0, 0.2),
     'L0_gnn_ln2_bias': (0.0, 0.1)}
    factors = {}
    for name, (base, spread) in spreads.items():
        noise = np.random.default_rng([zlib.crc32(name.encode()), seed]).standard_normal(out[name].shape)
        drawn = base * np.exp(spread * noise) if base else spread * noise
        out[name] = jnp.asarray(drawn.astype(out[name].dtype))
    for name, factor in factors.items():
        out[name] = (out[name] * factor).astype(out[name].dtype)
    return out
```

```python
from contextlib import ExitStack

import concourse.bass as bass
from concourse import mybir

F32 = mybir.dt.float32
F16 = mybir.dt.float16
BF16 = mybir.dt.bfloat16
I32 = mybir.dt.int32
ALU = mybir.AluOpType
ACT = mybir.ActivationFunctionType

P = 128
N = 2048
D = 256
H = 8
HD = D // H
F = 4 * D
NT = N // P
DC = D // P
FC = F // P
TB = 512
TT = TB // P
NTB = N // TB
UNITS = NTB * H
STEPS = NT
PAIRS = STEPS // 2
AHEAD = 3
SHIFT_ROW = 3 * HD
VW = 2 * HD + 1
VS = VW + 1
CTX_TB = TT * H * VW
BLK32 = TT * N // 2
NEG = -1e30
EPS = 1e-5
INV_SQRT_HD = float(HD) ** -0.5
SHIFT_MAX = 60000.0
CREDIT = 2
CTX0 = 2176
assert CTX0 >= CTX_TB and BLK32 >= CTX_TB and CTX0 % 2 == 0


def bcast_rows(vec):
    return vec.partition_broadcast(P)


def gnn_kernel(nc, x, adj, nodemask, h_target, ln1_scale, ln1_bias, Wq, bq, Wk, bk, Wv, bv, Wo, bo,
               ln2_scale, ln2_bias, W1, W2, out):
    with ExitStack() as top:
        def sb(stack, name, shape, dt):
            return stack.enter_context(nc.sbuf_tensor(name, shape, dt))

        def psum(stack, name, shape, dt=F32):
            return stack.enter_context(nc.psum_tensor(name, shape, dt))

        def sem(name):
            return top.enter_context(nc.semaphore(name))

        mask_ctx = sb(top, "mask_ctx", [P, CTX0 + NTB * BLK32], F32)
        mask_nat = mask_ctx[:, CTX0:].bitcast(BF16).rearrange("p (t s) -> p t s", s=N)
        node_f = sb(top, "node_f", [P, NT], F32)
        ht_mean = sb(top, "ht_mean", [P, NT], F32)
        ht_rstd = sb(top, "ht_rstd", [P, NT], F32)
        ident32 = sb(top, "ident32", [P, P], F32)
        ident16 = sb(top, "ident16", [P, P], F16)
        identb = sb(top, "identb", [P, P], BF16)

        attn_mem = ExitStack()
        kT = sb(attn_mem, "kT", [P, H, N], F16)
        qT = sb(attn_mem, "qT", [P, UNITS, TB], F16)
        v_sb = sb(attn_mem, "v_sb", [P, NT, H, VS], F16)

        prologue(nc, sb, psum, sem, locals())
        attention(nc, sb, psum, sem, locals())
        attn_mem.close()
        epilogue(nc, sb, psum, sem, locals())


def prologue(nc, sb, psum, sem, g):
    x, adj, nodemask, h_target = g["x"], g["adj"], g["nodemask"], g["h_target"]
    kT, qT, v_sb, mask_nat, node_f = g["kT"], g["qT"], g["v_sb"], g["mask_nat"], g["node_f"]
    ident32, ident16, identb = g["ident32"], g["ident16"], g["identb"]
    ht_mean, ht_rstd = g["ht_mean"], g["ht_rstd"]
    with ExitStack() as mem:
        src = qT[:, UNITS // 2:, :].bitcast(F32).rearrange("p u t -> p (u t)").rearrange("p (t d) -> p t d", d=D)
        tgt = sb(mem, "tgt", [P, NT, D], F32)
        adj_in = [sb(mem, f"adj_in{i}", [P, N], I32) for i in range(2)]
        wkv = sb(mem, "wkv", [P, DC, 2, D], F32)
        wq = sb(mem, "wq", [P, DC, D], F32)
        spare = g["mask_ctx"]
        bias_kv = spare[:, 0:2 * D].rearrange("p (k d) -> p k d", k=2)
        bias_q = spare[:, 2 * D:3 * D]
        normed = [spare[:, (3 + i) * D:(4 + i) * D] for i in range(2)]
        assert 5 * D <= CTX0
        ln1_g = sb(mem, "ln1_g", [P, DC], F32)
        ln1_b = sb(mem, "ln1_b", [P, DC], F32)
        node_i = sb(mem, "node_i", [P, NT], I32)
        nT = [sb(mem, f"nT{i}", [P, DC, P], F32) for i in range(2)]
        kvf = [sb(mem, f"kvf{i}", [P, 2, D], F32) for i in range(2)]
        stack = [sb(mem, f"stack{i}", [P, H, P], F16) for i in range(2)]
        stats = sb(mem, "stats", [P, NT, 6], F32)
        tmp = sb(mem, "tmp", [P, 4, NT], F32)
        s_mean = sb(mem, "s_mean", [P, NT], F32)
        s_rstd = sb(mem, "s_rstd", [P, NT], F32)
        s_shift = sb(mem, "s_shift", [P, NT], F32)
        deg = sb(mem, "deg", [P, NT], F32)
        q_scale = sb(mem, "q_scale", [P, NT], F32)
        neg_big = sb(mem, "neg_big", [P, NT], F32)

        tpose = [psum(mem, f"tpose{i}", [P, DC, P]) for i in range(2)]
        proj = [psum(mem, f"proj{i}", [P, 2, D]) for i in range(2)]
        stackT = [psum(mem, f"stackT{i}", [P, H, P], F16) for i in range(2)]

        WEIGHTS = 9 * 16
        src_in, tgt_in, wts_in = sem("src_in"), sem("tgt_in"), sem("wts_in")
        adj_in_sem = [sem(f"adj_in_sem{i}") for i in range(2)]
        consts = sem("consts")
        ident_made = sem("ident_made")
        stat_done, fin, var_ready, std_ready, rstd_ready = (
            sem("stat_done"), sem("fin"), sem("var_ready"), sem("std_ready"), sem("rstd_ready"))
        relu_done, norm_done = sem("relu_done"), sem("norm_done")
        tp_ready, nT_ready, proj_ready = sem("tp_ready"), sem("nT_ready"), sem("proj_ready")
        kv_ready, hi_ready, stack_ready, v_lo = sem("kv_ready"), sem("hi_ready"), sem("stack_ready"), sem("v_lo")
        stT_ready, stT_done = sem("stT_ready"), sem("stT_done")
        deg_ready, big_ready, mask_done = sem("deg_ready"), sem("big_ready"), sem("mask_done")
        q_raw = sem("q_raw")

        def heads(row):
            return row.rearrange("p (h d) -> p h d", h=H)

        def v_tile(n):
            return v_sb[:, bass.ds(n, 1), :, :].rearrange("p t h w -> p (t h) w")

        def mask_tile(n):
            return mask_nat[:, bass.ds(n, 1), :].rearrange("p t s -> p (t s)")

        with nc.Block() as block:
            @block.sync
            def _(sp):
                sp.dma_start(src, x.rearrange("(t p) d -> p t d", p=P)).then_inc(src_in, 16)
                sp.dma_start(tgt[:, :, :], h_target.rearrange("(t p) d -> p t d", p=P)).then_inc(tgt_in, 16)
                for i, w in enumerate((g["Wk"], g["Wv"])):
                    sp.dma_start(wkv[:, :, i, :], w.rearrange("(c p) n -> p c n", p=P)).then_inc(wts_in, 16)
                sp.dma_start(wq[:, :, :], g["Wq"].rearrange("(c p) n -> p c n", p=P)).then_inc(wts_in, 16)
                for i, b in enumerate((g["bk"], g["bv"])):
                    sp.dma_start(bias_kv[:, i, :], bcast_rows(b)).then_inc(wts_in, 16)
                sp.dma_start(bias_q[:, :], bcast_rows(g["bq"])).then_inc(wts_in, 16)
                with nc.allow_non_contiguous_dma(reason="small vectors, one element per partition"):
                    sp.dma_start(ln1_g[:, :], g["ln1_scale"].rearrange("(c p) -> p c", p=P)).then_inc(wts_in, 16)
                    sp.dma_start(ln1_b[:, :], g["ln1_bias"].rearrange("(c p) -> p c", p=P)).then_inc(wts_in, 16)
                    sp.dma_start(node_i[:, :], nodemask.rearrange("(t p) -> p t", p=P)).then_inc(wts_in, 16)
                adj_rows = adj.rearrange("(i two p) s -> p i two s", two=2, p=P)
                with sp.Fori(0, NT // 2) as i:
                    for b in range(2):
                        sp.wait_ge(mask_done, 2 * i + b + 1)
                        sp.dma_start(adj_in[b][:, :], adj_rows[:, bass.ds(i, 1), b, :]).then_inc(adj_in_sem[b], 16)

            @block.gpsimd
            def _(pool):
                for m in (ident32, ident16, identb):
                    nc.gpsimd.memset(m[:, :], 0.0).then_inc(ident_made, 1)
                pool.wait_ge(ident_made, 3)
                for m in (ident32, ident16, identb):
                    nc.gpsimd.affine_select(out=m[:, :], in_=m[:, :], compare_op=ALU.not_equal, fill=1.0, base=0,
                                            pattern=[[-1, P]], channel_multiplier=1).then_inc(ident_made, 1)
                for s in stack:
                    nc.gpsimd.memset(s[:, :, :], 0.0).then_inc(ident_made, 1)
                pool.wait_ge(ident_made, 8)
                for s in stack:
                    nc.gpsimd.memset(s[:, :, SHIFT_ROW:SHIFT_ROW + 1], 1.0).then_inc(ident_made, 1)
                nc.gpsimd.memset(v_sb[:, :, :, 2 * HD:VS], 1.0).then_inc(ident_made, 1)
                with pool.Fori(0, NT // 2) as i:
                    for b in range(2):
                        n = 2 * i + b
                        pool.wait_ge(hi_ready, n + 1)
                        nc.gpsimd.tensor_tensor(v_tile(n)[:, :, HD:2 * HD], heads(kvf[b][:, 1, :]),
                                                v_tile(n)[:, :, 0:HD], ALU.subtract).then_inc(v_lo, 1)

            @block.scalar
            def _(act):
                act.wait_ge(var_ready, 1)
                nc.scalar.activation(s_rstd[:, :], tmp[:, 3, :], ACT.Sqrt).then_inc(std_ready, 1)
                act.wait_ge(rstd_ready, 1)
                with act.Fori(0, NT) as i:
                    t = src[:, bass.ds(i, 1), :]
                    nc.scalar.activation(t, t, ACT.Relu, bias=s_shift[:, bass.ds(i, 1)],
                                         scale=s_rstd[:, bass.ds(i, 1)]).then_inc(relu_done, 1)
                for k in (2, 3):
                    act.wait_ge(var_ready, k)
                    dst = s_rstd if k == 2 else ht_rstd
                    nc.scalar.activation(dst[:, :], tmp[:, 3, :], ACT.Sqrt).then_inc(std_ready, 1)

                def features(n, b):
                    act.wait_ge(tp_ready, n + 1 + CREDIT)
                    act.wait_ge(proj_ready, n + 1)
                    for c in range(DC):
                        last = nc.scalar.activation(nT[b][:, c, :], tpose[b][:, c, :], ACT.Identity,
                                                    bias=ln1_b[:, c:c + 1], scale=ln1_g[:, c:c + 1])
                    last.then_inc(nT_ready, 1)

                def high_parts(n, b, kind):
                    act.wait_ge(kv_ready, n + 1 + CREDIT)
                    act.wait_ge(stT_ready, n + 1)
                    kq = heads(kvf[b][:, 0, :]).unsqueeze(2).to_broadcast([P, H, 2, HD])
                    st = stack[b][:, :, :].rearrange("p h (r d) -> p h r d", r=4)
                    if kind == "target":
                        nc.scalar.activation(st[:, :, 0:3:2, :], kq, ACT.Copy).then_inc(hi_ready, 1)
                        return
                    nc.scalar.activation(st[:, :, 0:2, :], kq, ACT.Copy)
                    nc.scalar.activation(v_tile(n)[:, :, 0:HD], heads(kvf[b][:, 1, :]), ACT.Copy).then_inc(hi_ready, 1)

                def degrees(n, b, i):
                    act.wait_ge(adj_in_sem[b], 16 * (i + 1))
                    nc.scalar.activation(mask_tile(n), adj_in[b][:, :], ACT.Square,
                                         accum_out=deg[:, bass.ds(n, 1)]).then_inc(deg_ready, 1)

                act.wait_ge(wts_in, WEIGHTS)
                features(0, 0)
                with act.Fori(0, NT // 2) as i:
                    for b in range(2):
                        n = 2 * i + b
                        features(n + 1, 1 - b)
                        degrees(n, b, i)
                        high_parts(n, b, "source")
                with act.Fori(NT // 2, NT - 1) as i:
                    for b in range(2):
                        features(2 * i + b + 1, 1 - b)
                        high_parts(2 * i + b, b, "target")
                features(2 * NT - 1, 1)
                for b in range(2):
                    high_parts(2 * NT - 2 + b, b, "target")

            @block.vector
            def _(dve):
                chain = [0]

                def link(ins):
                    chain[0] += 1
                    ins.then_inc(fin, 1)
                    dve.wait_ge(fin, chain[0])

                def spread(tiles, mean, done):
                    with dve.Fori(0, NT) as i:
                        nc.vector.bn_stats(stats[:, bass.ds(i, 1), :], tiles[:, bass.ds(i, 1), :]).then_inc(stat_done, 1)
                    dve.wait_ge(stat_done, NT * done)
                    me, qe, mo, qo = (stats[:, :, k] for k in (1, 2, 4, 5))
                    link(nc.vector.tensor_tensor(tmp[:, 0, :], me, mo, ALU.subtract))
                    link(nc.vector.tensor_tensor(tmp[:, 1, :], qe, qo, ALU.add))
                    link(nc.vector.tensor_tensor(tmp[:, 2, :], me, mo, ALU.add))
                    link(nc.vector.tensor_scalar(mean[:, :], tmp[:, 2, :], 0.5, None, ALU.mult))
                    link(nc.vector.tensor_tensor(tmp[:, 0, :], tmp[:, 0, :], tmp[:, 0, :], ALU.mult))
                    link(nc.vector.scalar_tensor_tensor(out=tmp[:, 1, :], in0=tmp[:, 0, :], scalar=D / 4.0,
                                                        in1=tmp[:, 1, :], op0=ALU.mult, op1=ALU.add))
                    nc.vector.tensor_scalar(tmp[:, 3, :], tmp[:, 1, :], 1.0 / D, EPS, ALU.mult, ALU.add).then_inc(var_ready, 1)

                def normalize(n, b, tiles, m, mean, rstd):
                    dve.wait_ge(tp_ready, n + 1)
                    nc.vector.tensor_scalar(normed[b][:, :], tiles[:, bass.ds(m, 1), :].rearrange("p t d -> p (t d)"),
                                            mean[:, bass.ds(m, 1)], rstd[:, bass.ds(m, 1)],
                                            ALU.subtract, ALU.mult).then_inc(norm_done, 1)

                dve.sem_inc(mask_done, CREDIT)
                dve.wait_ge(src_in, 16)
                spread(src, s_mean, 1)
                dve.wait_ge(std_ready, 1)
                link(nc.vector.reciprocal(s_rstd[:, :], s_rstd[:, :]))
                nc.vector.scalar_tensor_tensor(out=s_shift[:, :], in0=s_mean[:, :], scalar=-1.0, in1=s_rstd[:, :],
                                               op0=ALU.mult, op1=ALU.mult).then_inc(rstd_ready, 1)
                dve.wait_ge(wts_in, WEIGHTS)
                link(nc.vector.tensor_scalar(node_f[:, :], node_i[:, :], 1.0, None, ALU.is_equal))
                dve.wait_ge(relu_done, NT)
                spread(src, s_mean, 2)
                dve.wait_ge(std_ready, 2)
                link(nc.vector.reciprocal(s_rstd[:, :], s_rstd[:, :]))
                dve.wait_ge(tgt_in, 16)
                spread(tgt, ht_mean, 3)
                dve.wait_ge(std_ready, 3)
                link(nc.vector.reciprocal(ht_rstd[:, :], ht_rstd[:, :]))

                def project(n, b, kind):
                    dve.wait_ge(proj_ready, n + 1 + CREDIT)
                    dve.wait_ge(stack_ready, n + 1)
                    if kind == "source":
                        dve.wait_ge(v_lo, n + 1)
                        for k in range(2):
                            last = nc.vector.scalar_tensor_tensor(
                                out=kvf[b][:, k, :], in0=proj[b][:, k, :], scalar=node_f[:, bass.ds(n, 1)],
                                in1=bias_kv[:, k, :], op0=ALU.mult, op1=ALU.add)
                        last.then_inc(kv_ready, 1)
                        return
                    m = n - NT
                    dve.wait_ge(v_lo, NT + CREDIT)
                    nc.vector.scalar_tensor_tensor(out=kvf[b][:, 1, :], in0=proj[b][:, 0, :],
                                                   scalar=node_f[:, bass.ds(m, 1)], in1=bias_q[:, :],
                                                   op0=ALU.mult, op1=ALU.add).then_inc(q_raw, 1)
                    dve.wait_ge(q_raw, m + 1)
                    nc.vector.tensor_scalar(kvf[b][:, 0, :], kvf[b][:, 1, :], q_scale[:, bass.ds(m, 1)], None,
                                            ALU.mult).then_inc(kv_ready, 1)

                def make_mask(n, b):
                    nb = bass.ds(n, 1)
                    dve.wait_ge(deg_ready, n + 1)
                    nc.vector.tensor_scalar(neg_big[:, nb], deg[:, nb], 0.0, NEG, ALU.is_gt, ALU.mult).then_inc(big_ready, 1)
                    dve.wait_ge(big_ready, n + 1)
                    nc.vector.tensor_scalar(mask_tile(n), adj_in[b][:, :], 0.0, neg_big[:, nb],
                                            ALU.is_equal, ALU.mult).then_inc(mask_done, 1)

                def low_part(n, b, at):
                    dve.wait_ge(hi_ready, n + 1)
                    nc.vector.tensor_tensor(stack[b][:, :, at * HD:(at + 1) * HD], heads(kvf[b][:, 0, :]),
                                            stack[b][:, :, 0:HD], ALU.subtract).then_inc(stack_ready, 1)

                def stack_out(n, b, dst):
                    dve.wait_ge(stT_ready, n + 1 + CREDIT)
                    nc.vector.tensor_copy(dst, stackT[b][:, :, :]).then_inc(stT_done, 1)

                def k_place(n):
                    return kT[:, :, bass.ds(n * P, P)]

                def q_place(i, t):
                    return qT[:, bass.ds(i * H, H), t * P:(t + 1) * P]

                def source_tile(n, b):
                    project(n, b, "source")
                    make_mask(n, b)
                    low_part(n, b, 2)

                def norm_source(n, b):
                    normalize(n, b, src, n, s_mean, s_rstd)

                def norm_target(m, b):
                    normalize(m + NT, b, tgt, m, ht_mean, ht_rstd)

                for n in range(2):
                    norm_source(n, n)
                source_tile(0, 0)
                stack_out(0, 0, k_place(0))
                norm_source(2, 0)
                source_tile(1, 1)

                def later_source_tile(n, b, norm_next, m):
                    norm_next(m, 1 - b)
                    project(n, b, "source")
                    stack_out(n - 1, 1 - b, k_place(n - 1))
                    make_mask(n, b)
                    low_part(n, b, 2)

                with dve.Fori(1, NT // 2 - 1) as i:
                    for b in range(2):
                        later_source_tile(2 * i + b, b, norm_source, 2 * i + b + 1)
                later_source_tile(NT - 2, 0, norm_source, NT - 1)
                later_source_tile(NT - 1, 1, norm_target, 0)
                stack_out(NT - 1, 1, k_place(NT - 1))
                for s in stack:
                    link(nc.vector.memset(s[:, :, SHIFT_ROW:SHIFT_ROW + 1], 0.0))
                link(nc.vector.tensor_scalar(q_scale[:, :], deg[:, :], 0.0, INV_SQRT_HD, ALU.is_gt, ALU.mult))

                def target_tile(blk, t, more):
                    n = blk * TT + t + NT
                    if more:
                        norm_target(n + 1 - NT, 1 - t % 2)
                    project(n, t % 2, "target")
                    low_part(n, t % 2, 1)
                    stack_out(n, t % 2, q_place(blk, t))

                with dve.Fori(0, NTB - 1) as blk:
                    for t in range(TT):
                        target_tile(blk, t, True)
                for t in range(TT):
                    target_tile(NTB - 1, t, t < TT - 1)
                dve.wait_ge(stT_done, 2 * NT + CREDIT)

            @block.tensor
            def _(pe):
                for s in (nT_ready, proj_ready, kv_ready, stack_ready, stT_ready, stT_done, v_lo, tp_ready):
                    pe.sem_inc(s, CREDIT)
                pe.wait_ge(ident_made, 11)
                pe.wait_ge(wts_in, WEIGHTS)
                wkv_c = wkv[:, :, :, :].rearrange("p c k d -> p c (k d)")

                def turn(n, b):
                    pe.wait_ge(norm_done, n + 1)
                    pe.wait_ge(nT_ready, n + 1)
                    for c in range(DC):
                        last = nc.tensor.transpose(tpose[b][:, c, :], normed[b][:, c * P:(c + 1) * P], ident32[:, :])
                    last.then_inc(tp_ready, 1)

                def project(n, b, w, width):
                    pe.wait_ge(nT_ready, n + 1 + CREDIT)
                    pe.wait_ge(kv_ready, n + 1)
                    for c in range(DC):
                        last = nc.tensor.matmul(proj[b][:, 0:width, :].rearrange("p k d -> p (k d)"), nT[b][:, c, :],
                                                w[:, c, :], start=(c == 0), stop=(c == DC - 1))
                    last.then_inc(proj_ready, 1)

                def turn_stack(n, b):
                    pe.wait_ge(stack_ready, n + 1 + CREDIT)
                    pe.wait_ge(stT_done, n + 1)
                    for h in range(H):
                        last = nc.tensor.transpose(stackT[b][:, h, :], stack[b][:, h, :], ident16[:, :])
                    last.then_inc(stT_ready, 1)

                turn(0, 0)
                turn(1, 1)
                project(0, 0, wkv_c, 2)
                turn_stack(0, 0)
                turn(2, 0)
                project(1, 1, wkv_c, 2)
                with pe.Fori(1, NT // 2 - 1) as i:
                    for b in range(2):
                        n = 2 * i + b
                        turn(n + 1, 1 - b)
                        project(n, b, wkv_c, 2)
                        turn_stack(n - 1, 1 - b)
                for n in (NT - 2, NT - 1):
                    turn(n + 1, 1 - n % 2)
                    project(n, n % 2, wkv_c, 2)
                    turn_stack(n - 1, 1 - n % 2)
                turn_stack(NT - 1, 1)
                with pe.Fori(NT // 2, NT - 1) as i:
                    for b in range(2):
                        n = 2 * i + b
                        turn(n + 1, 1 - b)
                        project(n, b, wq[:, :, :], 1)
                        turn_stack(n, b)
                turn(2 * NT - 1, 1)
                for b in range(2):
                    project(2 * NT - 2 + b, b, wq[:, :, :], 1)
                    turn_stack(2 * NT - 2 + b, b)


def attention(nc, sb, psum, sem, g):
    kT, qT, v_sb, mask_nat, mask_ctx = g["kT"], g["qT"], g["v_sb"], g["mask_nat"], g["mask_ctx"]
    ident16, identb = g["ident16"], g["identb"]
    SLOTS = 4
    MASK_UNITS = UNITS - H
    PER_UNIT = NT // H
    LEAD = 2
    with ExitStack() as mem:
        mask_T = sb(mem, "mask_T", [P, 2, NT, TB], BF16)
        prob = sb(mem, "prob", [P, SLOTS, TB], F32)
        prob_lo = sb(mem, "prob_lo", [P, SLOTS, TB], F16)
        masked = [sb(mem, f"masked{i}", [P, N // 2], BF16) for i in range(2)]
        half_max = sb(mem, "half_max", [P, PAIRS], F32)
        row_max = sb(mem, "row_max", [P, TT], F32)
        shift = sb(mem, "shift", [P, TT, SHIFT_ROW + 1], F16)
        score = [psum(mem, f"score{i}", [P, TB]) for i in range(2)]
        early = [psum(mem, f"early{i}", [P, N // 2]) for i in range(2)]
        ctx = psum(mem, "ctx", [P, TT, VW])
        turned = psum(mem, "turned", [P, TB])
        turned_b = turned[:, :].bitcast(BF16)[:, 0:TB]

        score_ready = sem("score_ready")
        exp_done = sem("exp_done")
        lo_even, lo_odd = sem("lo_even"), sem("lo_odd")
        ctx_done = sem("ctx_done")
        ctx_out = sem("ctx_out")
        early_ready = sem("early_ready")
        max_done = sem("max_done")
        small = sem("small")
        shift_zero, shift_ready = sem("shift_zero"), sem("shift_ready")
        row_ready, row_done = sem("row_ready"), sem("row_done")
        mT_ready, mT_done = sem("mT_ready"), sem("mT_done")

        def prob_hi(slot):
            return prob[:, slot, :].bitcast(BF16).rearrange("p (t two) -> p t two", two=2)[:, :, 1]

        def every_unit(eng, unit):
            with eng.Fori(0, MASK_UNITS) as u:
                unit(u, True, True, True)
            with eng.Fori(MASK_UNITS, UNITS - LEAD) as u:
                unit(u, False, True, True)
            unit(UNITS - 2, False, False, True)
            unit(UNITS - 1, False, False, False)

        with nc.Block() as block:
            @block.tensor
            def _(pe):
                pe.sem_inc(ctx_done, SLOTS)

                def scores(u, m, at=None):
                    n = u * STEPS + m
                    if m == 0:
                        pe.wait_ge(row_done, u + 1)
                    pe.wait_ge(exp_done, n + 1)
                    nc.tensor.matmul(score[m % 2][:, :], kT[:, bass.ds(u % H, 1), m * P:(m + 1) * P],
                                     qT[:, bass.ds(u, 1), :], start=True, stop=False)
                    nc.tensor.matmul(score[m % 2][:, :], identb[:, :], mask_T[:, bass.ds((u // H) % 2, 1), m, :],
                                     start=False, stop=True).then_inc(score_ready, 1)

                def early_scores(w, s):
                    k, half = s // 2, s % 2
                    if half == 0:
                        pe.wait_ge(max_done, w * PAIRS + k + 1)
                    last = nc.tensor.matmul(early[k % 2][:, half * TB:(half + 1) * TB],
                                            qT[:, bass.ds(w, 1), (s // 4) * P:(s // 4 + 1) * P],
                                            kT[:, bass.ds(w % H, 1), (s % 4) * TB:(s % 4 + 1) * TB], start=True, stop=True)
                    if half == 1:
                        last.then_inc(early_ready, 1)

                def shift_row(w, masks):
                    pe.wait_ge(shift_ready, w + 1)
                    pe.wait_ge(mT_done, masks + 1)
                    for t in range(TT):
                        last = nc.tensor.matmul(turned[0:SHIFT_ROW + 1, t * P:(t + 1) * P], shift[:, t, :], ident16[:, :],
                                                start=True, stop=True)
                    last.then_inc(row_ready, 1)

                def turn_mask(blk, st, rows, masks):
                    if rows is not None:
                        pe.wait_ge(row_done, rows)
                    pe.wait_ge(mT_done, masks + 1)
                    for t in range(TT):
                        last = nc.tensor.transpose(
                            turned_b[:, t * P:(t + 1) * P],
                            mask_nat[:, bass.ds(blk * TT + t, 1), bass.ds(st * P, P)].rearrange("p t s -> p (t s)"),
                            identb[:, :])
                    last.then_inc(mT_ready, 1)

                def context(u, m):
                    n = u * STEPS + m
                    if m == 0:
                        pe.wait_ge(ctx_out, u + 1)
                    pe.wait_ge(lo_odd if m % 2 else lo_even, u * (STEPS // 2) + m // 2 + 1)
                    for t in range(TT):
                        cols = slice(t * P, (t + 1) * P)
                        v_h = v_sb[:, m, bass.ds(u % H, 1), 0:VW]
                        nc.tensor.matmul(ctx[:, t, :], prob_hi(m % SLOTS)[:, cols], v_h, start=(m == 0 and t == 0),
                                         stop=False, skip_group_check=True)
                        last = nc.tensor.matmul(ctx[:, t, :], prob_lo[:, m % SLOTS, cols], v_h, start=False,
                                                stop=(m == STEPS - 1), skip_group_check=True)
                    last.then_inc(ctx_done, 1)

                with pe.Fori(0, NT) as st:
                    turn_mask(0, st, None, st)
                pe.wait_ge(shift_zero, 1)
                for s in range(STEPS):
                    early_scores(0, s)
                shift_row(0, NT)
                for s in range(STEPS):
                    early_scores(1, s)
                for m in range(AHEAD):
                    scores(0, m)

                def unit(u, mask, early_too, more):
                    turned_before = NT + PER_UNIT * u if mask else NT * NTB
                    for s in range(STEPS):
                        if s + AHEAD < STEPS:
                            scores(u, s + AHEAD)
                        elif more:
                            scores(u + 1, s + AHEAD - STEPS)
                        if early_too:
                            for q in ([0, 1] if s == 0 else [s + 1] if s + 1 < STEPS else []):
                                early_scores(u + LEAD, q)
                        context(u, s)
                        if s == 4 and more:
                            shift_row(u + 1, turned_before)
                        if mask and s in (7, 11):
                            k = (s - 7) // 4
                            turn_mask(u // H + 1, (u % H) * PER_UNIT + k, u + 2, turned_before + k)

                every_unit(pe, unit)

            @block.scalar
            def _(act):
                def exponential(u, m):
                    n = u * STEPS + m
                    act.wait_ge(score_ready, n + 1)
                    act.wait_ge(ctx_done, n + 1)
                    nc.scalar.activation(prob[:, m % SLOTS, :], score[m % 2][:, :], ACT.Exp).then_inc(exp_done, 1)

                def mask_out(j, buf, st):
                    act.wait_ge(mT_ready, j + 1)
                    nc.scalar.activation(mask_T[:, bass.ds(buf, 1), bass.ds(st, 1), :].rearrange("p b s t -> p (b s t)"),
                                         turned_b, ACT.Copy).then_inc(mT_done, 1)

                def row_out(w):
                    act.wait_ge(row_ready, w + 1)
                    nc.scalar.activation(qT[SHIFT_ROW:SHIFT_ROW + 1, bass.ds(w, 1), :].rearrange("p u t -> p (u t)"),
                                         turned[SHIFT_ROW:SHIFT_ROW + 1, :], ACT.Copy).then_inc(row_done, 1)

                def context_out(u):
                    act.wait_ge(ctx_done, (u + 1) * STEPS + SLOTS)
                    dst = mask_ctx[:, bass.ds((u // H) * BLK32, CTX_TB)].rearrange("p (t h w) -> p t h w", t=TT, h=H)
                    nc.scalar.activation(dst[:, :, bass.ds(u % H, 1), :].rearrange("p t h w -> p t (h w)"), ctx[:, :, :],
                                         ACT.Copy).then_inc(ctx_out, 1)

                act.sem_inc(exp_done, 2)
                act.sem_inc(ctx_out, 1)
                act.sem_inc(mT_done, 1)
                with act.Fori(0, NT) as st:
                    mask_out(st, 0, st)
                row_out(0)
                for m in range(AHEAD):
                    exponential(0, m)

                def unit(u, mask, early_too, more):
                    for s in range(STEPS):
                        if s + AHEAD < STEPS:
                            exponential(u, s + AHEAD)
                        elif more:
                            exponential(u + 1, s + AHEAD - STEPS)
                        if s == 5 and more:
                            row_out(u + 1)
                        if mask and s in (8, 12):
                            k = (s - 8) // 4
                            mask_out(NT + PER_UNIT * u + k, (u // H + 1) % 2, (u % H) * PER_UNIT + k)
                    context_out(u)

                every_unit(act, unit)

            def low_part(eng, u, m, done):
                eng.wait_ge(exp_done, u * STEPS + m + 3)
                eng.tensor_tensor(prob_lo[:, m % SLOTS, :], prob[:, m % SLOTS, :], prob_hi(m % SLOTS),
                                  ALU.subtract).then_inc(done, 1)

            @block.gpsimd
            def _(pool):
                low_part(nc.gpsimd, 0, 1, lo_odd)
                low_part(nc.gpsimd, 0, 3, lo_odd)

                def unit(u, mask, early_too, more):
                    for m in range(5, STEPS + 4, 2):
                        if m < STEPS:
                            low_part(nc.gpsimd, u, m, lo_odd)
                        elif more:
                            low_part(nc.gpsimd, u + 1, m - STEPS, lo_odd)

                every_unit(pool, unit)

            @block.vector
            def _(dve):
                def maxima(w, k, blk):
                    dve.wait_ge(early_ready, w * PAIRS + k + 1)
                    dve.wait_ge(max_done, w * PAIRS + k + 1)
                    dve.nop(nofuse=True)
                    half = slice((k % 2) * (N // 2), (k % 2 + 1) * (N // 2))
                    nc.vector.tensor_tensor_reduce(out=masked[k % 2][:, :], in0=early[k % 2][:, :],
                                                   in1=mask_nat[:, blk * TT + k // 2, half], scale=1.0, scalar=-3.0e38,
                                                   op0=ALU.add, op1=ALU.max, accum_out=half_max[:, k:k + 1]).then_inc(max_done, 1)

                def negated(w):
                    dve.wait_ge(max_done, (w + 1) * PAIRS + 2)
                    pair = half_max[:, :].rearrange("p (t two) -> p t two", two=2)
                    nc.vector.tensor_tensor(row_max[:, :], pair[:, :, 0], pair[:, :, 1], ALU.max).then_inc(small, 1)
                    dve.wait_ge(small, w + 1)
                    if not (isinstance(w, int) and w == 0):
                        dve.wait_ge(row_ready, w)
                    nc.vector.tensor_scalar(shift[:, :, SHIFT_ROW], row_max[:, :], -1.0, -SHIFT_MAX, ALU.mult,
                                            ALU.max).then_inc(shift_ready, 1)

                dve.sem_inc(max_done, 2)
                nc.vector.memset(shift[:, :, :], 0.0).then_inc(shift_zero, 1)
                dve.wait_ge(shift_zero, 1)
                for w in range(LEAD):
                    for k in range(PAIRS):
                        maxima(w, k, 0)
                    negated(w)
                for m in (0, 2):
                    low_part(nc.vector, 0, m, lo_even)

                def unit(u, blk, more):
                    for k in range(PAIRS):
                        if blk is not None:
                            maxima(u + LEAD, k, blk)
                        m = 2 * k + 4
                        if m < STEPS:
                            low_part(nc.vector, u, m, lo_even)
                        elif more:
                            low_part(nc.vector, u + 1, m - STEPS, lo_even)
                    if blk is not None:
                        negated(u + LEAD)

                for blk in range(NTB):
                    with dve.Fori(max(blk * H - LEAD, 0), (blk + 1) * H - LEAD) as u:
                        unit(u, blk, True)
                unit(UNITS - 2, None, True)
                unit(UNITS - 1, None, False)


def epilogue(nc, sb, psum, sem, g):
    mask_ctx, node_f, ht_mean, ht_rstd, ident32 = (
        g["mask_ctx"], g["node_f"], g["ht_mean"], g["ht_rstd"], g["ident32"])
    with ExitStack() as mem:
        res = sb(mem, "res", [P, NT, D], F32)
        xin = sb(mem, "xin", [P, NT, D], F32)
        wo = sb(mem, "wo", [P, DC, D], F32)
        w1 = sb(mem, "w1", [P, DC, F], F32)
        w2 = sb(mem, "w2", [P, FC, D], F32)
        vecs = sb(mem, "vecs", [P, 5, D], F32)
        rden = sb(mem, "rden", [P, TT * H], F32)
        h2 = sb(mem, "h2", [P, TT, D], F32)
        csum = sb(mem, "csum", [P, TT * H, HD], F32)
        cnorm = sb(mem, "cnorm", [P, TT, D], F32)
        fT = sb(mem, "fT", [P, DC, TB], F32)
        act_T = sb(mem, "act_T", [P, FC, TB], F32)
        yout = [sb(mem, f"yout{i}", [P, D], F32) for i in range(2)]
        stats = sb(mem, "stats2", [P, NT, 6], F32)
        tmp = sb(mem, "tmp2", [P, 4, NT], F32)
        mean = sb(mem, "mean2", [P, NT], F32)
        rstd = sb(mem, "rstd2", [P, NT], F32)
        tp = [psum(mem, f"tp{c}", [P, TB]) for c in range(DC)]
        row = [psum(mem, f"row{i}", [P, D]) for i in range(2)]
        up = [psum(mem, f"up{i}", [P, TB]) for i in range(2)]

        loads, link_s = sem("loads"), sem("link_s")
        cn_sum, cn_ready, y_ready = sem("cn_sum"), sem("cn_ready"), sem("y_ready")
        rden_ready = sem("rden_ready")
        tp_r, fT_r, row_r, row_f = sem("tp_r"), sem("fT_r"), sem("row_r"), sem("row_f")
        var2, std2, stat2 = sem("var2"), sem("std2"), sem("stat2")
        h2_ready, res_ready = sem("h2_ready"), sem("res_ready")
        up_r, gelu_r = sem("up_r"), sem("gelu_r")
        y_out, stored = sem("y_out"), [sem(f"stored{i}") for i in range(2)]
        LOADS = 10 * 16

        def rows(t4):
            return bass.ds(t4 * TT, TT)

        with nc.Block() as block:
            @block.sync
            def _(sp):
                sp.dma_start(res[:, :, :], g["h_target"].rearrange("(t p) d -> p t d", p=P)).then_inc(loads, 16)
                sp.dma_start(wo[:, :, :], g["Wo"].rearrange("(c p) n -> p c n", p=P)).then_inc(loads, 16)
                for i, v in enumerate(("ln1_scale", "ln1_bias", "bo", "ln2_scale", "ln2_bias")):
                    sp.dma_start(vecs[:, i, :], bcast_rows(g[v])).then_inc(loads, 16)
                sp.dma_start(w1[:, :, :], g["W1"].rearrange("(c p) n -> p c n", p=P)).then_inc(loads, 16)
                sp.dma_start(w2[:, :, :], g["W2"].rearrange("(c p) n -> p c n", p=P)).then_inc(loads, 16)
                sp.dma_start(xin[:, :, :], g["x"].rearrange("(t p) d -> p t d", p=P)).then_inc(loads, 16)
                out_rows = g["out"].rearrange("(i two p) d -> p i two d", two=2, p=P)
                with sp.Fori(0, NT // 2) as i:
                    for b in range(2):
                        sp.wait_ge(y_out, 2 * i + b + 1 + CREDIT)
                        sp.dma_start(out_rows[:, bass.ds(i, 1), b, :], yout[b][:, :]).then_inc(stored[b], 16)
                for b in range(2):
                    sp.wait_ge(stored[b], (NT // 2) * 16)

            @block.gpsimd
            def _(pool):
                with pool.Fori(0, NTB) as k:
                    raw = mask_ctx[:, bass.ds(k * BLK32, CTX_TB)].rearrange("p (a w) -> p a w", w=VW)
                    pool.wait_ge(cn_ready, k + 1)
                    nc.gpsimd.tensor_tensor(csum[:, :, :], raw[:, :, 0:HD], raw[:, :, HD:2 * HD], ALU.add).then_inc(cn_sum, 1)
                    pool.wait_ge(cn_sum, k + 1)
                    pool.wait_ge(rden_ready, k + 1)
                    pool.wait_ge(tp_r, DC * k + 1)
                    nc.gpsimd.tensor_tensor(cnorm[:, :, :].rearrange("p t (h d) -> p (t h) d", h=H), csum[:, :, :],
                                            rden[:, :].unsqueeze(2).to_broadcast([P, TT * H, HD]),
                                            ALU.mult).then_inc(cn_ready, 1)
                with pool.Fori(0, NTB) as k:
                    pool.wait_ge(h2_ready, k + 1)
                    nc.gpsimd.tensor_tensor(xin[:, rows(k), :], xin[:, rows(k), :], h2[:, :, :],
                                            ALU.add).then_inc(res_ready, 1)

            @block.scalar
            def _(act):
                def turned_out(k, products, ups):
                    for c in range(DC):
                        act.wait_ge(tp_r, DC * k + c + 2)
                        if c == 0:
                            act.wait_ge(row_r, products + 1)
                            act.wait_ge(up_r, ups + 1)
                        nc.scalar.activation(fT[:, c, :], tp[c][:, :], ACT.Copy).then_inc(fT_r, 1)

                with act.Fori(0, NTB) as k:
                    turned_out(k, TT * k, 0)
                act.wait_ge(var2, 1)
                nc.scalar.activation(rstd[:, :], tmp[:, 3, :], ACT.Sqrt).then_inc(std2, 1)
                with act.Fori(0, NTB) as k:
                    turned_out(k + NTB, NT, FC * k)
                    for f in range(FC):
                        act.wait_ge(up_r, FC * k + f + 2)
                        if f == 0:
                            act.wait_ge(row_r, NT + TT * k + 1)
                        nc.scalar.activation(act_T[:, f, :], up[f % 2][:, :], ACT.Gelu_apprx_tanh).then_inc(gelu_r, 1)

            @block.vector
            def _(dve):
                chain = [0]

                def link(ins):
                    chain[0] += 1
                    ins.then_inc(link_s, 1)
                    dve.wait_ge(link_s, chain[0])

                def spread(scalars, shape):
                    return scalars.unsqueeze(len(scalars.shape)).to_broadcast(shape)

                def per_tile(vec):
                    return vec.unsqueeze(1).to_broadcast([P, NT, D])

                dve.wait_ge(loads, LOADS)
                all_rows = [P, NT, D]
                link(nc.vector.tensor_tensor(res[:, :, :], res[:, :, :], spread(ht_mean[:, :], all_rows), ALU.subtract))
                link(nc.vector.tensor_tensor(res[:, :, :], res[:, :, :], spread(ht_rstd[:, :], all_rows), ALU.mult))
                link(nc.vector.tensor_tensor(res[:, :, :], res[:, :, :], per_tile(vecs[:, 0, :]), ALU.mult))
                link(nc.vector.tensor_tensor(res[:, :, :], res[:, :, :], per_tile(vecs[:, 1, :]), ALU.add))
                link(nc.vector.tensor_tensor(res[:, :, :], res[:, :, :], per_tile(vecs[:, 2, :]), ALU.add))
                with dve.Fori(0, NTB) as k:
                    raw = mask_ctx[:, bass.ds(k * BLK32, CTX_TB)].rearrange("p (a w) -> p a w", w=VW)
                    dve.wait_ge(cn_ready, k + 1)
                    nc.vector.reciprocal(rden[:, :], raw[:, :, VW - 1]).then_inc(rden_ready, 1)
                    for t in range(TT):
                        n = k * TT + t
                        nb = bass.ds(n, 1)
                        dve.wait_ge(row_r, n + 2)
                        row_t = res[:, nb, :].rearrange("p t d -> p (t d)")
                        nc.vector.tensor_tensor(row_t, row[t % 2][:, :], row_t, ALU.add).then_inc(row_f, 1)
                        dve.wait_ge(row_f, n + 1 + CREDIT)
                        nc.vector.tensor_scalar(row_t, row_t, node_f[:, nb], None, ALU.mult).then_inc(y_ready, 1)
                        dve.wait_ge(y_ready, n + 1)
                        nc.vector.bn_stats(stats[:, nb, :], row_t).then_inc(stat2, 1)
                dve.wait_ge(stat2, NT)
                me, qe, mo, qo = (stats[:, :, i] for i in (1, 2, 4, 5))
                link(nc.vector.tensor_tensor(tmp[:, 0, :], me, mo, ALU.subtract))
                link(nc.vector.tensor_tensor(tmp[:, 1, :], qe, qo, ALU.add))
                link(nc.vector.tensor_tensor(tmp[:, 2, :], me, mo, ALU.add))
                link(nc.vector.tensor_scalar(mean[:, :], tmp[:, 2, :], 0.5, None, ALU.mult))
                link(nc.vector.tensor_tensor(tmp[:, 0, :], tmp[:, 0, :], tmp[:, 0, :], ALU.mult))
                link(nc.vector.scalar_tensor_tensor(out=tmp[:, 1, :], in0=tmp[:, 0, :], scalar=D / 4.0,
                                                    in1=tmp[:, 1, :], op0=ALU.mult, op1=ALU.add))
                nc.vector.tensor_scalar(tmp[:, 3, :], tmp[:, 1, :], 1.0 / D, EPS, ALU.mult, ALU.add).then_inc(var2, 1)
                dve.wait_ge(std2, 1)
                link(nc.vector.reciprocal(rstd[:, :], rstd[:, :]))

                def second_norm(k):
                    r = res[:, k * TT:(k + 1) * TT, :]
                    block_rows = [P, TT, D]
                    ts = slice(k * TT, (k + 1) * TT)
                    for vec, op in ((spread(mean[:, ts], block_rows), ALU.subtract), (spread(rstd[:, ts], block_rows), ALU.mult),
                                    (vecs[:, 3, :].unsqueeze(1).to_broadcast(block_rows), ALU.mult),
                                    (vecs[:, 4, :].unsqueeze(1).to_broadcast(block_rows), ALU.add)):
                        link(nc.vector.tensor_tensor(r, r, vec, op))
                    dve.wait_ge(tp_r, DC * (k + NTB) + 1)
                    if k > 0:
                        dve.wait_ge(res_ready, k)
                    nc.vector.tensor_tensor(h2[:, :, :], r, spread(node_f[:, ts], block_rows), ALU.mult).then_inc(h2_ready, 1)

                def store_rows(k):
                    dve.wait_ge(res_ready, k + 1)
                    for t in range(TT):
                        b, n = t % 2, k * TT + t
                        i = k * (TT // 2) + t // 2
                        dve.wait_ge(row_r, NT + n + 2)
                        if i > 0:
                            dve.wait_ge(stored[b], 16 * i)
                        nc.vector.tensor_tensor(yout[b][:, :], row[b][:, :], xin[:, n, :], ALU.add).then_inc(y_out, 1)

                second_norm(0)
                for k in range(NTB):
                    if k + 1 < NTB:
                        second_norm(k + 1)
                    store_rows(k)

            @block.tensor
            def _(pe):
                for s in (row_f, y_out, gelu_r):
                    pe.sem_inc(s, CREDIT)
                for s in (cn_ready, tp_r, fT_r, row_r, up_r):
                    pe.sem_inc(s, 1)

                def turn(j, tile):
                    pe.wait_ge(fT_r, DC * j + 1)
                    for c in range(DC):
                        for t in range(TT):
                            last = nc.tensor.transpose(tp[c][:, t * P:(t + 1) * P], tile(t, c), ident32[:, :])
                        last.then_inc(tp_r, 1)

                pe.wait_ge(loads, LOADS)
                with pe.Fori(0, NTB) as k:
                    pe.wait_ge(cn_ready, k + 2)
                    turn(k, lambda t, c: cnorm[:, t, c * P:(c + 1) * P])
                    pe.wait_ge(fT_r, DC * (k + 1) + 1)
                    for t in range(TT):
                        pe.wait_ge(row_f, k * TT + t + 1)
                        for c in range(DC):
                            last = nc.tensor.matmul(row[t % 2][:, :], fT[:, c, t * P:(t + 1) * P], wo[:, c, :],
                                                    start=(c == 0), stop=(c == DC - 1))
                        last.then_inc(row_r, 1)
                pe.wait_ge(row_f, NT + CREDIT)
                with pe.Fori(0, NTB) as k:
                    pe.wait_ge(h2_ready, k + 1)
                    turn(k + NTB, lambda t, c: h2[:, t, c * P:(c + 1) * P])
                    pe.wait_ge(fT_r, DC * (k + NTB + 1) + 1)
                    for f in range(FC):
                        pe.wait_ge(gelu_r, FC * k + f + 1)
                        for c in range(DC):
                            last = nc.tensor.matmul(up[f % 2][:, :], w1[:, c, f * P:(f + 1) * P], fT[:, c, :],
                                                    start=(c == 0), stop=(c == DC - 1))
                        last.then_inc(up_r, 1)
                    pe.wait_ge(gelu_r, FC * (k + 1) + CREDIT)
                    for t in range(TT):
                        pe.wait_ge(y_out, k * TT + t + 1)
                        for f in range(FC):
                            last = nc.tensor.matmul(row[t % 2][:, :], act_T[:, f, t * P:(t + 1) * P], w2[:, f, :],
                                                    start=(f == 0), stop=(f == FC - 1))
                        last.then_inc(row_r, 1)


_INS = ["x", "adj", "nodemask", "L0_gnn_h_target", "L0_gnn_ln1_scale", "L0_gnn_ln1_bias", "L0_gnn_Wq", "L0_gnn_bq",
        "L0_gnn_Wk", "L0_gnn_bk", "L0_gnn_Wv", "L0_gnn_bv", "L0_gnn_Wo", "L0_gnn_bo", "L0_gnn_ln2_scale",
        "L0_gnn_ln2_bias", "L0_gnn_W1", "L0_gnn_W2"]


def kernel(**inputs):
    import numpy as np
    import concourse.bacc as bacc
    from concourse import mybir as mb
    from concourse.bass_utils import run_bass_kernel_spmd

    nc = bacc.Bacc("TRN2", target_bir_lowering=False, num_devices=1)
    arrays, args = {}, []
    for name in _INS:
        a = np.ascontiguousarray(inputs[name])
        arrays[f"in_{name}"] = a
        args.append(nc.dram_tensor(f"in_{name}", a.shape, mb.dt.from_np(a.dtype), kind="ExternalInput").ap())
    out = nc.dram_tensor("out_y", (N, D), mb.dt.from_np(np.dtype("float32")), kind="ExternalOutput").ap()
    gnn_kernel(nc, *args, out)
    r = run_bass_kernel_spmd(nc, [arrays], core_ids=[0])
    return r.results[0]["out_y"]
```

```python
from contextlib import ExitStack

import concourse.bass as bass
from concourse import mybir

F32 = mybir.dt.float32
F16 = mybir.dt.float16
BF16 = mybir.dt.bfloat16
I32 = mybir.dt.int32
ALU = mybir.AluOpType
ACT = mybir.ActivationFunctionType

P = 128
N = 2048
D = 256
H = 8
HD = D // H
F = 4 * D
NT = N // P
DC = D // P
FC = F // P
TB = 512
TT = TB // P
NTB = N // TB
UNITS = NTB * H
STEPS = NT
PAIRS = STEPS // 2
AHEAD = 3
SHIFT_ROW = 3 * HD
VW = 2 * HD + 1
VS = VW + 1
CTX_TB = TT * H * VW
BLK32 = TT * N // 2
NEG = -1e30
EPS = 1e-5
INV_SQRT_HD = float(HD) ** -0.5
SHIFT_MAX = 60000.0
CREDIT = 2
CTX0 = 2176
assert CTX0 >= CTX_TB and BLK32 >= CTX_TB + TT * D and CTX0 % 2 == 0


def bcast_rows(vec):
    return vec.partition_broadcast(P)


def gnn_kernel(nc, x, adj, nodemask, h_target, ln1_scale, ln1_bias, Wq, bq, Wk, bk, Wv, bv, Wo, bo,
               ln2_scale, ln2_bias, W1, W2, out):
    with ExitStack() as top:
        def sb(stack, name, shape, dt):
            return stack.enter_context(nc.sbuf_tensor(name, shape, dt))

        def psum(stack, name, shape, dt=F32):
            return stack.enter_context(nc.psum_tensor(name, shape, dt))

        def sem(name):
            return top.enter_context(nc.semaphore(name))

        mask_ctx = sb(top, "mask_ctx", [P, CTX0 + NTB * BLK32], F32)
        mask_nat = mask_ctx[:, CTX0:].bitcast(BF16).rearrange("p (t s) -> p t s", s=N)
        node_f = sb(top, "node_f", [P, NT], F32)
        ht_shift = sb(top, "ht_shift", [P, NT], F32)
        ht_rstd = sb(top, "ht_rstd", [P, NT], F32)
        ident32 = sb(top, "ident32", [P, P], F32)
        ident16 = sb(top, "ident16", [P, P], F16)
        identb = sb(top, "identb", [P, P], BF16)

        weights = sb(top, "weights", [P, (DC + 5) * D], F32)
        wo = weights[:, :DC * D].rearrange("p (c d) -> p c d", c=DC)
        vecs = weights[:, DC * D:].rearrange("p (k d) -> p k d", k=5)

        attn_mem = ExitStack()
        kT = sb(attn_mem, "kT", [P, H, N], F16)
        qT = sb(attn_mem, "qT", [P, UNITS, TB], F16)
        v_sb = sb(attn_mem, "v_sb", [P, NT, H, VS], F16)

        prologue(nc, sb, psum, sem, locals())
        attention(nc, sb, psum, sem, locals())
        attn_mem.close()
        epilogue(nc, sb, psum, sem, locals())


def prologue(nc, sb, psum, sem, g):
    x, adj, nodemask, h_target = g["x"], g["adj"], g["nodemask"], g["h_target"]
    kT, qT, v_sb, mask_nat, node_f = g["kT"], g["qT"], g["v_sb"], g["mask_nat"], g["node_f"]
    ident32, ident16, identb = g["ident32"], g["ident16"], g["identb"]
    ht_shift, ht_rstd = g["ht_shift"], g["ht_rstd"]
    with ExitStack() as mem:
        src = qT[:, UNITS // 2:, :].bitcast(F32).rearrange("p u t -> p (u t)").rearrange("p (t d) -> p t d", d=D)
        tgt = sb(mem, "tgt", [P, NT, D], F32)
        adj_in = [sb(mem, f"adj_in{i}", [P, N], I32) for i in range(2)]
        wkv = g["weights"][:, :2 * DC * D].rearrange("p (c k d) -> p c k d", c=DC, k=2)
        wq = g["weights"][:, 2 * DC * D:3 * DC * D].rearrange("p (c d) -> p c d", c=DC)
        spare = g["mask_ctx"]
        bias_kv = spare[:, 0:2 * D].rearrange("p (k d) -> p k d", k=2)
        bias_q = spare[:, 2 * D:3 * D]
        normed = [spare[:, (3 + i) * D:(4 + i) * D] for i in range(2)]
        assert 5 * D <= CTX0
        ln1_g = sb(mem, "ln1_g", [P, DC], F32)
        ln1_b = sb(mem, "ln1_b", [P, DC], F32)
        node_i = sb(mem, "node_i", [P, NT], I32)
        nT = [sb(mem, f"nT{i}", [P, DC, P], F32) for i in range(2)]
        kvf = [sb(mem, f"kvf{i}", [P, 2, D], F32) for i in range(2)]
        stack = [sb(mem, f"stack{i}", [P, H, P], F16) for i in range(2)]
        stats = sb(mem, "stats", [P, NT, 6], F32)
        tmp = sb(mem, "tmp", [P, 4, NT], F32)
        ht_mean = sb(mem, "ht_mean", [P, NT], F32)
        s_mean = sb(mem, "s_mean", [P, NT], F32)
        s_rstd = sb(mem, "s_rstd", [P, NT], F32)
        s_shift = sb(mem, "s_shift", [P, NT], F32)
        deg = sb(mem, "deg", [P, NT], F32)
        q_scale = sb(mem, "q_scale", [P, NT], F32)
        neg_big = sb(mem, "neg_big", [P, NT], F32)

        tpose = [psum(mem, f"tpose{i}", [P, DC, P]) for i in range(2)]
        proj = [psum(mem, f"proj{i}", [P, 2, D]) for i in range(2)]
        stackT = [psum(mem, f"stackT{i}", [P, H, P], F16) for i in range(2)]

        WEIGHTS = 9 * 16
        src_in, tgt_in, wts_in = sem("src_in"), sem("tgt_in"), sem("wts_in")
        adj_in_sem = [sem(f"adj_in_sem{i}") for i in range(2)]
        consts = sem("consts")
        ident_made = sem("ident_made")
        stat_done, fin, var_ready, std_ready, rstd_ready = (
            sem("stat_done"), sem("fin"), sem("var_ready"), sem("std_ready"), sem("rstd_ready"))
        relu_done, norm_done = sem("relu_done"), sem("norm_done")
        tp_ready, nT_ready, proj_ready = sem("tp_ready"), sem("nT_ready"), sem("proj_ready")
        kv_ready, hi_ready, stack_ready, v_lo = sem("kv_ready"), sem("hi_ready"), sem("stack_ready"), sem("v_lo")
        stT_ready, stT_done = sem("stT_ready"), sem("stT_done")
        deg_ready, big_ready, mask_done = sem("deg_ready"), sem("big_ready"), sem("mask_done")
        q_raw = sem("q_raw")

        def heads(row):
            return row.rearrange("p (h d) -> p h d", h=H)

        def v_tile(n):
            return v_sb[:, bass.ds(n, 1), :, :].rearrange("p t h w -> p (t h) w")

        def mask_tile(n):
            return mask_nat[:, bass.ds(n, 1), :].rearrange("p t s -> p (t s)")

        with nc.Block() as block:
            @block.sync
            def _(sp):
                sp.dma_start(src, x.rearrange("(t p) d -> p t d", p=P)).then_inc(src_in, 16)
                sp.dma_start(tgt[:, :, :], h_target.rearrange("(t p) d -> p t d", p=P)).then_inc(tgt_in, 16)
                for i, w in enumerate((g["Wk"], g["Wv"])):
                    sp.dma_start(wkv[:, :, i, :], w.rearrange("(c p) n -> p c n", p=P)).then_inc(wts_in, 16)
                sp.dma_start(wq[:, :, :], g["Wq"].rearrange("(c p) n -> p c n", p=P)).then_inc(wts_in, 16)
                for i, b in enumerate((g["bk"], g["bv"])):
                    sp.dma_start(bias_kv[:, i, :], bcast_rows(b)).then_inc(wts_in, 16)
                sp.dma_start(bias_q[:, :], bcast_rows(g["bq"])).then_inc(wts_in, 16)
                with nc.allow_non_contiguous_dma(reason="small vectors, one element per partition"):
                    sp.dma_start(ln1_g[:, :], g["ln1_scale"].rearrange("(c p) -> p c", p=P)).then_inc(wts_in, 16)
                    sp.dma_start(ln1_b[:, :], g["ln1_bias"].rearrange("(c p) -> p c", p=P)).then_inc(wts_in, 16)
                    sp.dma_start(node_i[:, :], nodemask.rearrange("(t p) -> p t", p=P)).then_inc(wts_in, 16)
                adj_rows = adj.rearrange("(i two p) s -> p i two s", two=2, p=P)
                with sp.Fori(0, NT // 2) as i:
                    for b in range(2):
                        sp.wait_ge(mask_done, 2 * i + b + 1)
                        sp.dma_start(adj_in[b][:, :], adj_rows[:, bass.ds(i, 1), b, :]).then_inc(adj_in_sem[b], 16)

            @block.gpsimd
            def _(pool):
                for m in (ident32, ident16, identb):
                    nc.gpsimd.memset(m[:, :], 0.0).then_inc(ident_made, 1)
                pool.wait_ge(ident_made, 3)
                for m in (ident32, ident16, identb):
                    nc.gpsimd.affine_select(out=m[:, :], in_=m[:, :], compare_op=ALU.not_equal, fill=1.0, base=0,
                                            pattern=[[-1, P]], channel_multiplier=1).then_inc(ident_made, 1)
                for s in stack:
                    nc.gpsimd.memset(s[:, :, :], 0.0).then_inc(ident_made, 1)
                pool.wait_ge(ident_made, 8)
                for s in stack:
                    nc.gpsimd.memset(s[:, :, SHIFT_ROW:SHIFT_ROW + 1], 1.0).then_inc(ident_made, 1)
                nc.gpsimd.memset(v_sb[:, :, :, 2 * HD:VS], 1.0).then_inc(ident_made, 1)
                with pool.Fori(0, NT // 2) as i:
                    for b in range(2):
                        n = 2 * i + b
                        pool.wait_ge(hi_ready, n + 1)
                        nc.gpsimd.tensor_tensor(v_tile(n)[:, :, HD:2 * HD], heads(kvf[b][:, 1, :]),
                                                v_tile(n)[:, :, 0:HD], ALU.subtract).then_inc(v_lo, 1)

            @block.scalar
            def _(act):
                act.wait_ge(var_ready, 1)
                nc.scalar.activation(s_rstd[:, :], tmp[:, 3, :], ACT.Sqrt).then_inc(std_ready, 1)
                act.wait_ge(rstd_ready, 1)
                with act.Fori(0, NTB) as i:
                    for t in range(TT):
                        nb = bass.ds(i * TT + t, 1)
                        nc.scalar.activation(src[:, nb, :], src[:, nb, :], ACT.Relu, bias=s_shift[:, nb],
                                             scale=s_rstd[:, nb]).then_inc(relu_done, 1)
                for k in (2, 3):
                    act.wait_ge(var_ready, k)
                    dst = ht_rstd if k == 2 else s_rstd
                    nc.scalar.activation(dst[:, :], tmp[:, 3, :], ACT.Sqrt).then_inc(std_ready, 1)

                def features(n, b):
                    act.wait_ge(tp_ready, n + 1 + CREDIT)
                    act.wait_ge(proj_ready, n + 1)
                    for c in range(DC):
                        last = nc.scalar.activation(nT[b][:, c, :], tpose[b][:, c, :], ACT.Identity,
                                                    bias=ln1_b[:, c:c + 1], scale=ln1_g[:, c:c + 1])
                    last.then_inc(nT_ready, 1)

                def high_parts(n, b, kind):
                    act.wait_ge(kv_ready, n + 1 + CREDIT)
                    act.wait_ge(stT_ready, n + 1)
                    kq = heads(kvf[b][:, 0, :]).unsqueeze(2).to_broadcast([P, H, 2, HD])
                    st = stack[b][:, :, :].rearrange("p h (r d) -> p h r d", r=4)
                    if kind == "target":
                        nc.scalar.activation(st[:, :, 0:3:2, :], kq, ACT.Copy).then_inc(hi_ready, 1)
                        return
                    nc.scalar.activation(st[:, :, 0:2, :], kq, ACT.Copy)
                    nc.scalar.activation(v_tile(n)[:, :, 0:HD], heads(kvf[b][:, 1, :]), ACT.Copy).then_inc(hi_ready, 1)

                def degrees(n, b, i):
                    act.wait_ge(adj_in_sem[b], 16 * (i + 1))
                    nc.scalar.activation(mask_tile(n), adj_in[b][:, :], ACT.Square,
                                         accum_out=deg[:, bass.ds(n, 1)]).then_inc(deg_ready, 1)

                act.wait_ge(wts_in, WEIGHTS)
                features(0, 0)
                with act.Fori(0, NT // 2) as i:
                    for b in range(2):
                        n = 2 * i + b
                        features(n + 1, 1 - b)
                        high_parts(n, b, "source")
                        degrees(n, b, i)
                with act.Fori(NT // 2, NT - 1) as i:
                    for b in range(2):
                        features(2 * i + b + 1, 1 - b)
                        high_parts(2 * i + b, b, "target")
                features(2 * NT - 1, 1)
                for b in range(2):
                    high_parts(2 * NT - 2 + b, b, "target")

            @block.vector
            def _(dve):
                chain = [0]

                def link(ins):
                    chain[0] += 1
                    ins.then_inc(fin, 1)
                    dve.wait_ge(fin, chain[0])

                def spread(tiles, mean, done):
                    with dve.Fori(0, NTB) as i:
                        for t in range(TT):
                            nb = bass.ds(i * TT + t, 1)
                            nc.vector.bn_stats(stats[:, nb, :], tiles[:, nb, :]).then_inc(stat_done, 1)
                    dve.wait_ge(stat_done, NT * done)
                    me, qe, mo, qo = (stats[:, :, k] for k in (1, 2, 4, 5))
                    link(nc.vector.tensor_tensor(tmp[:, 0, :], me, mo, ALU.subtract))
                    link(nc.vector.tensor_tensor(tmp[:, 1, :], qe, qo, ALU.add))
                    link(nc.vector.tensor_tensor(tmp[:, 2, :], me, mo, ALU.add))
                    link(nc.vector.tensor_scalar(mean[:, :], tmp[:, 2, :], 0.5, None, ALU.mult))
                    link(nc.vector.tensor_tensor(tmp[:, 0, :], tmp[:, 0, :], tmp[:, 0, :], ALU.mult))
                    link(nc.vector.scalar_tensor_tensor(out=tmp[:, 1, :], in0=tmp[:, 0, :], scalar=D / 4.0,
                                                        in1=tmp[:, 1, :], op0=ALU.mult, op1=ALU.add))
                    nc.vector.tensor_scalar(tmp[:, 3, :], tmp[:, 1, :], 1.0 / D, EPS, ALU.mult, ALU.add).then_inc(var_ready, 1)

                def normalize(n, b, tiles, m, mean, rstd):
                    dve.wait_ge(tp_ready, n + 1)
                    nc.vector.tensor_scalar(normed[b][:, :], tiles[:, bass.ds(m, 1), :].rearrange("p t d -> p (t d)"),
                                            mean[:, bass.ds(m, 1)], rstd[:, bass.ds(m, 1)],
                                            ALU.subtract, ALU.mult).then_inc(norm_done, 1)

                dve.sem_inc(mask_done, CREDIT)
                dve.wait_ge(src_in, 16)
                spread(src, s_mean, 1)
                dve.wait_ge(std_ready, 1)
                link(nc.vector.reciprocal(s_rstd[:, :], s_rstd[:, :]))
                nc.vector.scalar_tensor_tensor(out=s_shift[:, :], in0=s_mean[:, :], scalar=-1.0, in1=s_rstd[:, :],
                                               op0=ALU.mult, op1=ALU.mult).then_inc(rstd_ready, 1)
                dve.wait_ge(wts_in, WEIGHTS)
                link(nc.vector.tensor_scalar(node_f[:, :], node_i[:, :], 1.0, None, ALU.is_equal))
                dve.wait_ge(tgt_in, 16)
                spread(tgt, ht_mean, 2)
                dve.wait_ge(std_ready, 2)
                link(nc.vector.reciprocal(ht_rstd[:, :], ht_rstd[:, :]))
                nc.vector.scalar_tensor_tensor(out=ht_shift[:, :], in0=ht_mean[:, :], scalar=-1.0, in1=ht_rstd[:, :],
                                               op0=ALU.mult, op1=ALU.mult)
                dve.wait_ge(relu_done, NT)
                spread(src, s_mean, 3)
                dve.wait_ge(std_ready, 3)
                link(nc.vector.reciprocal(s_rstd[:, :], s_rstd[:, :]))

                def project(n, b, kind):
                    dve.wait_ge(proj_ready, n + 1 + CREDIT)
                    dve.wait_ge(stack_ready, n + 1)
                    if kind == "source":
                        dve.wait_ge(v_lo, n + 1)
                        for k in range(2):
                            last = nc.vector.scalar_tensor_tensor(
                                out=kvf[b][:, k, :], in0=proj[b][:, k, :], scalar=node_f[:, bass.ds(n, 1)],
                                in1=bias_kv[:, k, :], op0=ALU.mult, op1=ALU.add)
                        last.then_inc(kv_ready, 1)
                        return
                    m = n - NT
                    dve.wait_ge(v_lo, NT + CREDIT)
                    nc.vector.scalar_tensor_tensor(out=kvf[b][:, 1, :], in0=proj[b][:, 0, :],
                                                   scalar=node_f[:, bass.ds(m, 1)], in1=bias_q[:, :],
                                                   op0=ALU.mult, op1=ALU.add).then_inc(q_raw, 1)
                    dve.wait_ge(q_raw, m + 1)
                    nc.vector.tensor_scalar(kvf[b][:, 0, :], kvf[b][:, 1, :], q_scale[:, bass.ds(m, 1)], None,
                                            ALU.mult).then_inc(kv_ready, 1)

                def make_mask(n, b):
                    nb = bass.ds(n, 1)
                    dve.wait_ge(deg_ready, n + 1)
                    nc.vector.tensor_scalar(neg_big[:, nb], deg[:, nb], 0.0, NEG, ALU.is_gt, ALU.mult).then_inc(big_ready, 1)
                    dve.wait_ge(big_ready, n + 1)
                    nc.vector.tensor_scalar(mask_tile(n), adj_in[b][:, :], 0.0, neg_big[:, nb],
                                            ALU.is_equal, ALU.mult).then_inc(mask_done, 1)

                def low_part(n, b, at):
                    dve.wait_ge(hi_ready, n + 1)
                    nc.vector.tensor_tensor(stack[b][:, :, at * HD:(at + 1) * HD], heads(kvf[b][:, 0, :]),
                                            stack[b][:, :, 0:HD], ALU.subtract).then_inc(stack_ready, 1)

                def stack_out(n, b, dst):
                    dve.wait_ge(stT_ready, n + 1 + CREDIT)
                    nc.vector.tensor_copy(dst, stackT[b][:, :, :]).then_inc(stT_done, 1)

                def k_place(n):
                    return kT[:, :, bass.ds(n * P, P)]

                def q_place(i, t):
                    return qT[:, bass.ds(i * H, H), t * P:(t + 1) * P]

                def source_tile(n, b, norm_ahead, out_before=True):
                    norm_ahead(n + 2, b)
                    project(n, b, "source")
                    if out_before:
                        make_mask(n - 1, 1 - b)
                        stack_out(n - 1, 1 - b, k_place(n - 1))
                    low_part(n, b, 2)

                def norm_source(n, b):
                    normalize(n, b, src, n, s_mean, s_rstd)

                def norm_target(n, b):
                    normalize(n, b, tgt, n - NT, ht_mean, ht_rstd)

                for n in range(2):
                    norm_source(n, n)
                source_tile(0, 0, norm_source, False)
                source_tile(1, 1, norm_source)
                with dve.Fori(1, NT // 2 - 1) as i:
                    for b in range(2):
                        source_tile(2 * i + b, b, norm_source)
                for b in range(2):
                    source_tile(NT - 2 + b, b, norm_target)
                make_mask(NT - 1, 1)
                link(nc.vector.tensor_scalar(q_scale[:, :], deg[:, :], 0.0, INV_SQRT_HD, ALU.is_gt, ALU.mult))

                def target_tile(blk, t, before, ahead=True):
                    b = t % 2
                    n = blk * TT + t + NT
                    if ahead:
                        norm_target(n + 2, b)
                    project(n, b, "target")
                    stack_out(n - 1, 1 - b, before)
                    if isinstance(blk, int) and blk == 0 and t < 2:
                        link(nc.vector.memset(stack[b][:, :, SHIFT_ROW:SHIFT_ROW + 1], 0.0))
                    low_part(n, b, 1)

                def target_block(blk, first, ahead=TT):
                    for t in range(TT):
                        target_tile(blk, t, first if t == 0 else q_place(blk, t - 1), t < ahead)

                target_block(0, k_place(NT - 1))
                with dve.Fori(1, NTB - 1) as blk:
                    target_block(blk, q_place(blk - 1, TT - 1))
                target_block(NTB - 1, q_place(NTB - 2, TT - 1), TT - 2)
                stack_out(2 * NT - 1, 1, q_place(NTB - 1, TT - 1))
                dve.wait_ge(stT_done, 2 * NT + CREDIT)

            @block.tensor
            def _(pe):
                for s in (nT_ready, proj_ready, kv_ready, stack_ready, stT_ready, stT_done, v_lo, tp_ready):
                    pe.sem_inc(s, CREDIT)
                pe.wait_ge(ident_made, 11)
                pe.wait_ge(wts_in, WEIGHTS)
                wkv_c = wkv[:, :, :, :].rearrange("p c k d -> p c (k d)")

                def turn(n, b):
                    pe.wait_ge(norm_done, n + 1)
                    pe.wait_ge(nT_ready, n + 1)
                    for c in range(DC):
                        last = nc.tensor.transpose(tpose[b][:, c, :], normed[b][:, c * P:(c + 1) * P], ident32[:, :])
                    last.then_inc(tp_ready, 1)

                def project(n, b, w, width):
                    pe.wait_ge(nT_ready, n + 1 + CREDIT)
                    pe.wait_ge(kv_ready, n + 1)
                    for c in range(DC):
                        last = nc.tensor.matmul(proj[b][:, 0:width, :].rearrange("p k d -> p (k d)"), nT[b][:, c, :],
                                                w[:, c, :], start=(c == 0), stop=(c == DC - 1))
                    last.then_inc(proj_ready, 1)

                def turn_stack(n, b):
                    pe.wait_ge(stack_ready, n + 1 + CREDIT)
                    pe.wait_ge(stT_done, n + 1)
                    for h in range(H):
                        last = nc.tensor.transpose(stackT[b][:, h, :], stack[b][:, h, :], ident16[:, :])
                    last.then_inc(stT_ready, 1)

                def step(n, b, w, width, first=False, ahead=True):
                    if ahead:
                        turn(n + 1, 1 - b)
                    project(n, b, w, width)
                    if not first:
                        turn_stack(n - 1, 1 - b)

                kv, q = (wkv_c, 2), (wq[:, :, :], 1)
                turn(0, 0)
                step(0, 0, *kv, first=True)
                step(1, 1, *kv)
                with pe.Fori(1, NT // 2) as i:
                    for b in range(2):
                        step(2 * i + b, b, *kv)
                with pe.Fori(NT // 2, NT - 1) as i:
                    for b in range(2):
                        step(2 * i + b, b, *q)
                for b in range(2):
                    step(2 * NT - 2 + b, b, *q, ahead=b == 0)
                turn_stack(2 * NT - 1, 1)


def attention(nc, sb, psum, sem, g):
    kT, qT, v_sb, mask_nat, mask_ctx = g["kT"], g["qT"], g["v_sb"], g["mask_nat"], g["mask_ctx"]
    ident16, identb = g["ident16"], g["identb"]
    SLOTS = 4
    MASK_UNITS = UNITS - H
    PER_UNIT = NT // H
    LEAD = 2
    with ExitStack() as mem:
        mask_T = sb(mem, "mask_T", [P, 2, NT, TB], BF16)
        prob = sb(mem, "prob", [P, SLOTS, TB], F32)
        prob_lo = sb(mem, "prob_lo", [P, SLOTS, TB], F16)
        masked = g["weights"][:, DC * D:DC * D + N // 2].bitcast(BF16).rearrange("p (i s) -> p i s", i=2)
        half_max = sb(mem, "half_max", [P, PAIRS], F32)
        row_max = sb(mem, "row_max", [P, TT], F32)
        shift = sb(mem, "shift", [P, TT, SHIFT_ROW + 1], F16)
        score = [psum(mem, f"score{i}", [P, TB]) for i in range(2)]
        early = [psum(mem, f"early{i}", [P, N // 2]) for i in range(2)]
        ctx = psum(mem, "ctx", [P, TT, VW])
        turned = psum(mem, "turned", [P, TB])
        turned_b = turned[:, :].bitcast(BF16)[:, 0:TB]

        score_ready = sem("score_ready")
        exp_done = sem("exp_done")
        lo_even, lo_odd = sem("lo_even"), sem("lo_odd")
        ctx_done = sem("ctx_done")
        ctx_out = sem("ctx_out")
        early_ready = sem("early_ready")
        max_done = sem("max_done")
        small = sem("small")
        shift_zero, shift_ready = sem("shift_zero"), sem("shift_ready")
        row_ready, row_done = sem("row_ready"), sem("row_done")
        next_in = sem("next_in")
        mT_ready, mT_done = sem("mT_ready"), sem("mT_done")

        def prob_hi(slot):
            return prob[:, slot, :].bitcast(BF16).rearrange("p (t two) -> p t two", two=2)[:, :, 1]

        def every_unit(eng, unit):
            with eng.Fori(0, MASK_UNITS) as u:
                unit(u, True, True, True)
            with eng.Fori(MASK_UNITS, UNITS - LEAD) as u:
                unit(u, False, True, True)
            unit(UNITS - 2, False, False, True)
            unit(UNITS - 1, False, False, False)

        with nc.Block() as block:
            @block.sync
            def _(sp):
                sp.dma_start(g["wo"][:, :, :], g["Wo"].rearrange("(c p) n -> p c n", p=P)).then_inc(next_in, 16)
                sp.wait_ge(max_done, UNITS * PAIRS + 2)
                for i, v in enumerate(("ln1_scale", "ln1_bias", "bo", "ln2_scale", "ln2_bias")):
                    sp.dma_start(g["vecs"][:, i, :], bcast_rows(g[v])).then_inc(next_in, 16)
                for k in range(NTB):
                    at = k * BLK32 + CTX_TB
                    sp.dma_start(mask_ctx[:, at:at + TT * D].rearrange("p (t d) -> p t d", d=D),
                                 g["h_target"][k * TB:(k + 1) * TB, :].rearrange("(t p) d -> p t d", p=P)).then_inc(next_in, 16)
                sp.wait_ge(next_in, (6 + NTB) * 16)

            @block.tensor
            def _(pe):
                pe.sem_inc(ctx_done, SLOTS)

                def scores(u, m, at=None):
                    n = u * STEPS + m
                    if m == 0:
                        pe.wait_ge(row_done, u + 1)
                    pe.wait_ge(exp_done, n + 1)
                    nc.tensor.matmul(score[m % 2][:, :], kT[:, bass.ds(u % H, 1), m * P:(m + 1) * P],
                                     qT[:, bass.ds(u, 1), :], start=True, stop=False)
                    nc.tensor.matmul(score[m % 2][:, :], identb[:, :], mask_T[:, bass.ds((u // H) % 2, 1), m, :],
                                     start=False, stop=True).then_inc(score_ready, 1)

                def early_scores(w, s):
                    k, half = s // 2, s % 2
                    if half == 0:
                        pe.wait_ge(max_done, w * PAIRS + k + 1)
                    last = nc.tensor.matmul(early[k % 2][:, half * TB:(half + 1) * TB],
                                            qT[:, bass.ds(w, 1), (s // 4) * P:(s // 4 + 1) * P],
                                            kT[:, bass.ds(w % H, 1), (s % 4) * TB:(s % 4 + 1) * TB], start=True, stop=True)
                    if half == 1:
                        last.then_inc(early_ready, 1)

                def shift_row(w, masks):
                    pe.wait_ge(shift_ready, w + 1)
                    pe.wait_ge(mT_done, masks + 1)
                    for t in range(TT):
                        last = nc.tensor.matmul(turned[0:SHIFT_ROW + 1, t * P:(t + 1) * P], shift[:, t, :], ident16[:, :],
                                                start=True, stop=True)
                    last.then_inc(row_ready, 1)

                def turn_mask(blk, st, rows, masks):
                    if rows is not None:
                        pe.wait_ge(row_done, rows)
                    pe.wait_ge(mT_done, masks + 1)
                    for t in range(TT):
                        last = nc.tensor.transpose(
                            turned_b[:, t * P:(t + 1) * P],
                            mask_nat[:, bass.ds(blk * TT + t, 1), bass.ds(st * P, P)].rearrange("p t s -> p (t s)"),
                            identb[:, :])
                    last.then_inc(mT_ready, 1)

                def context(u, m):
                    n = u * STEPS + m
                    if m == 0:
                        pe.wait_ge(ctx_out, u + 1)
                    pe.wait_ge(lo_odd if m % 2 else lo_even, u * (STEPS // 2) + m // 2 + 1)
                    for t in range(TT):
                        cols = slice(t * P, (t + 1) * P)
                        v_h = v_sb[:, m, bass.ds(u % H, 1), 0:VW]
                        nc.tensor.matmul(ctx[:, t, :], prob_hi(m % SLOTS)[:, cols], v_h, start=(m == 0 and t == 0),
                                         stop=False, skip_group_check=True)
                        last = nc.tensor.matmul(ctx[:, t, :], prob_lo[:, m % SLOTS, cols], v_h, start=False,
                                                stop=(m == STEPS - 1), skip_group_check=True)
                    last.then_inc(ctx_done, 1)

                pe.wait_ge(shift_zero, 1)
                for s in range(STEPS):
                    early_scores(0, s)
                    turn_mask(0, s, None, s)
                shift_row(0, NT)
                for s in range(STEPS):
                    early_scores(1, s)
                for m in range(AHEAD):
                    scores(0, m)

                def unit(u, mask, early_too, more):
                    turned_before = NT + PER_UNIT * u if mask else NT * NTB
                    for s in range(STEPS):
                        if s + AHEAD < STEPS:
                            scores(u, s + AHEAD)
                        elif more:
                            scores(u + 1, s + AHEAD - STEPS)
                        if early_too:
                            for q in ([0, 1] if s == 0 else [s + 1] if s + 1 < STEPS else []):
                                early_scores(u + LEAD, q)
                        context(u, s)
                        if s == 4 and more:
                            shift_row(u + 1, turned_before)
                        if mask and s in (7, 11):
                            k = (s - 7) // 4
                            turn_mask(u // H + 1, (u % H) * PER_UNIT + k, u + 2, turned_before + k)

                every_unit(pe, unit)

            @block.scalar
            def _(act):
                def exponential(u, m):
                    n = u * STEPS + m
                    act.wait_ge(score_ready, n + 1)
                    act.wait_ge(ctx_done, n + 1)
                    nc.scalar.activation(prob[:, m % SLOTS, :], score[m % 2][:, :], ACT.Exp).then_inc(exp_done, 1)

                def mask_out(j, buf, st):
                    act.wait_ge(mT_ready, j + 1)
                    nc.scalar.activation(mask_T[:, bass.ds(buf, 1), bass.ds(st, 1), :].rearrange("p b s t -> p (b s t)"),
                                         turned_b, ACT.Copy).then_inc(mT_done, 1)

                def row_out(w):
                    act.wait_ge(row_ready, w + 1)
                    nc.scalar.activation(qT[SHIFT_ROW:SHIFT_ROW + 1, bass.ds(w, 1), :].rearrange("p u t -> p (u t)"),
                                         turned[SHIFT_ROW:SHIFT_ROW + 1, :], ACT.Copy).then_inc(row_done, 1)

                def context_out(u):
                    act.wait_ge(ctx_done, (u + 1) * STEPS + SLOTS)
                    dst = mask_ctx[:, bass.ds((u // H) * BLK32, CTX_TB)].rearrange("p (t h w) -> p t h w", t=TT, h=H)
                    nc.scalar.activation(dst[:, :, bass.ds(u % H, 1), :].rearrange("p t h w -> p t (h w)"), ctx[:, :, :],
                                         ACT.Copy).then_inc(ctx_out, 1)

                act.sem_inc(exp_done, 2)
                act.sem_inc(ctx_out, 1)
                act.sem_inc(mT_done, 1)
                with act.Fori(0, NT) as st:
                    mask_out(st, 0, st)
                row_out(0)
                for m in range(AHEAD):
                    exponential(0, m)

                def unit(u, mask, early_too, more):
                    for s in range(STEPS):
                        if s + AHEAD < STEPS:
                            exponential(u, s + AHEAD)
                        elif more:
                            exponential(u + 1, s + AHEAD - STEPS)
                        if s == 5 and more:
                            row_out(u + 1)
                        if mask and s in (8, 12):
                            k = (s - 8) // 4
                            mask_out(NT + PER_UNIT * u + k, (u // H + 1) % 2, (u % H) * PER_UNIT + k)
                    context_out(u)

                every_unit(act, unit)

            def low_part(eng, u, m, done):
                eng.wait_ge(exp_done, u * STEPS + m + 3)
                eng.tensor_tensor(prob_lo[:, m % SLOTS, :], prob[:, m % SLOTS, :], prob_hi(m % SLOTS),
                                  ALU.subtract).then_inc(done, 1)

            @block.gpsimd
            def _(pool):
                low_part(nc.gpsimd, 0, 1, lo_odd)
                low_part(nc.gpsimd, 0, 3, lo_odd)

                def unit(u, mask, early_too, more):
                    for m in range(5, STEPS + 4, 2):
                        if m < STEPS:
                            low_part(nc.gpsimd, u, m, lo_odd)
                        elif more:
                            low_part(nc.gpsimd, u + 1, m - STEPS, lo_odd)

                every_unit(pool, unit)

            @block.vector
            def _(dve):
                def maxima(w, k, blk):
                    dve.wait_ge(early_ready, w * PAIRS + k + 1)
                    dve.wait_ge(max_done, w * PAIRS + k + 1)
                    dve.nop(nofuse=True)
                    half = slice((k % 2) * (N // 2), (k % 2 + 1) * (N // 2))
                    nc.vector.tensor_tensor_reduce(out=masked[:, k % 2, :], in0=early[k % 2][:, :],
                                                   in1=mask_nat[:, blk * TT + k // 2, half], scale=1.0, scalar=-3.0e38,
                                                   op0=ALU.add, op1=ALU.max, accum_out=half_max[:, k:k + 1]).then_inc(max_done, 1)

                def negated(w):
                    dve.wait_ge(max_done, (w + 1) * PAIRS + 2)
                    pair = half_max[:, :].rearrange("p (t two) -> p t two", two=2)
                    nc.vector.tensor_tensor(row_max[:, :], pair[:, :, 0], pair[:, :, 1], ALU.max).then_inc(small, 1)
                    dve.wait_ge(small, w + 1)
                    if not (isinstance(w, int) and w == 0):
                        dve.wait_ge(row_ready, w)
                    nc.vector.tensor_scalar(shift[:, :, SHIFT_ROW], row_max[:, :], -1.0, -SHIFT_MAX, ALU.mult,
                                            ALU.max).then_inc(shift_ready, 1)

                dve.sem_inc(max_done, 2)
                nc.vector.memset(shift[:, :, :], 0.0).then_inc(shift_zero, 1)
                dve.wait_ge(shift_zero, 1)
                for w in range(LEAD):
                    for k in range(PAIRS):
                        maxima(w, k, 0)
                    negated(w)
                for m in (0, 2):
                    low_part(nc.vector, 0, m, lo_even)

                def unit(u, blk, more):
                    for k in range(PAIRS):
                        if blk is not None:
                            maxima(u + LEAD, k, blk)
                        m = 2 * k + 4
                        if m < STEPS:
                            low_part(nc.vector, u, m, lo_even)
                        elif more:
                            low_part(nc.vector, u + 1, m - STEPS, lo_even)
                    if blk is not None:
                        negated(u + LEAD)

                for blk in range(NTB):
                    with dve.Fori(max(blk * H - LEAD, 0), (blk + 1) * H - LEAD) as u:
                        unit(u, blk, True)
                unit(UNITS - 2, None, True)
                unit(UNITS - 1, None, False)


def epilogue(nc, sb, psum, sem, g):
    mask_ctx, node_f, ht_shift, ht_rstd, ident32 = (
        g["mask_ctx"], g["node_f"], g["ht_shift"], g["ht_rstd"], g["ident32"])
    wo, vecs = g["wo"], g["vecs"]
    LN1_G, LN1_B, BO, LN2_G, LN2_B = range(5)
    with ExitStack() as mem:
        xin = sb(mem, "xin", [P, NT, D], F32)
        w1 = sb(mem, "w1", [P, DC, F], F32)
        w2 = sb(mem, "w2", [P, FC, D], F32)
        w1_hi, w1_lo = (sb(mem, f"w1_{p}", [P, DC, F], F16) for p in ("hi", "lo"))
        w2_hi, w2_lo = (sb(mem, f"w2_{p}", [P, FC, D], F16) for p in ("hi", "lo"))
        rden = sb(mem, "rden", [P, TT * H], F32)
        csum = sb(mem, "csum", [P, TT * H, HD], F32)
        cnorm = sb(mem, "cnorm", [P, TT, D], F32)
        cT = sb(mem, "cT", [P, DC, TB], F32)
        h2 = sb(mem, "h2", [P, TT, D], F32)
        h2_hi, h2_lo = (sb(mem, f"h2_{p}", [P, DC, TB], F16) for p in ("hi", "lo"))
        gelu = sb(mem, "gelu", [P, 2, TB], F32)
        g_hi, g_lo = (sb(mem, f"g_{p}", [P, 2, FC, TB], F16) for p in ("hi", "lo"))
        yout = [sb(mem, f"yout{i}", [P, D], F32) for i in range(2)]
        stats = sb(mem, "stats2", [P, NT, 6], F32)
        tmp = sb(mem, "tmp2", [P, 4, NT], F32)
        mean = sb(mem, "mean2", [P, NT], F32)
        rstd = sb(mem, "rstd2", [P, NT], F32)
        tp = [psum(mem, f"tp{c}", [P, TB]) for c in range(DC)]
        row = [psum(mem, f"row{i}", [P, D]) for i in range(2)]
        up = [psum(mem, f"up{i}", [P, TB]) for i in range(2)]

        w1_in, w2_in, x_in = sem("w1_in"), sem("w2_in"), sem("x_in")
        link_s, bias_ready = sem("link_s"), sem("bias_ready")
        centred, scaled, ht_ready = sem("centred"), sem("scaled"), sem("ht_ready")
        csum_ready, cn_ready = sem("csum_ready"), sem("cn_ready")
        tp_ready2, cT_ready, row_ready2, row_read = sem("tp_ready2"), sem("cT_ready"), sem("row_ready2"), sem("row_read")
        stat2, var2, std2 = sem("stat2"), sem("var2"), sem("std2")
        w_hi, w1_split, w2_split = sem("w_hi"), sem("w1_split"), sem("w2_split")
        h2_ready, res_ready = sem("h2_ready"), sem("res_ready")
        h2_hi_ready, h2_lo_ready = sem("h2_hi_ready"), sem("h2_lo_ready")
        up_ready, gelu_ready, g_hi_ready, g_lo_ready = (
            sem("up_ready"), sem("gelu_ready"), sem("g_hi_ready"), sem("g_lo_ready"))
        y_out, stored = sem("y_out"), [sem(f"stored{i}") for i in range(2)]

        def raw(k):
            return mask_ctx[:, bass.ds(k * BLK32, CTX_TB)].rearrange("p (a w) -> p a w", w=VW)

        def res(k):
            return mask_ctx[:, bass.ds(k * BLK32 + CTX_TB, TT * D)].rearrange("p (t d) -> p t d", d=D)

        with nc.Block() as block:
            @block.sync
            def _(sp):
                sp.dma_start(w1[:, :, :], g["W1"].rearrange("(c p) n -> p c n", p=P)).then_inc(w1_in, 16)
                sp.dma_start(w2[:, :, :], g["W2"].rearrange("(c p) n -> p c n", p=P)).then_inc(w2_in, 16)
                sp.dma_start(xin[:, :, :], g["x"].rearrange("(t p) d -> p t d", p=P)).then_inc(x_in, 16)
                out_rows = g["out"].rearrange("(i two p) d -> p i two d", two=2, p=P)
                with sp.Fori(0, NT // 2) as i:
                    for b in range(2):
                        sp.wait_ge(y_out, 2 * i + b + 1 + CREDIT)
                        sp.dma_start(out_rows[:, bass.ds(i, 1), b, :], yout[b][:, :]).then_inc(stored[b], 16)
                for b in range(2):
                    sp.wait_ge(stored[b], (NT // 2) * 16)

            @block.gpsimd
            def _(pool):
                def wide(i):
                    return vecs[:, i, :].unsqueeze(1).to_broadcast([P, TT, D])

                nc.gpsimd.tensor_tensor(vecs[:, LN1_B, :], vecs[:, LN1_B, :], vecs[:, BO, :], ALU.add).then_inc(bias_ready, 1)
                pool.wait_ge(bias_ready, 1)
                for k in range(NTB):
                    pool.wait_ge(centred, TT * (k + 1))
                    nc.gpsimd.tensor_tensor(res(k), res(k), wide(LN1_G), ALU.mult).then_inc(scaled, 1)
                    pool.wait_ge(scaled, k + 1)
                    nc.gpsimd.tensor_tensor(res(k), res(k), wide(LN1_B), ALU.add).then_inc(ht_ready, 1)
                pool.wait_ge(w_hi, 1)
                nc.gpsimd.tensor_tensor(w1_lo[:, :, :], w1[:, :, :], w1_hi[:, :, :], ALU.subtract).then_inc(w1_split, 1)
                pool.wait_ge(w_hi, 2)
                nc.gpsimd.tensor_tensor(w2_lo[:, :, :], w2[:, :, :], w2_hi[:, :, :], ALU.subtract).then_inc(w2_split, 1)
                pool.wait_ge(x_in, 16)
                for k in range(NTB):
                    pool.wait_ge(h2_ready, k + 1)
                    nc.gpsimd.tensor_tensor(xin[:, bass.ds(k * TT, TT), :], xin[:, bass.ds(k * TT, TT), :], h2[:, :, :],
                                            ALU.add).then_inc(res_ready, 1)

            @block.scalar
            def _(act):
                def centre(k):
                    for t in range(TT):
                        nb = bass.ds(k * TT + t, 1)
                        r = mask_ctx[:, bass.ds(k * BLK32 + CTX_TB + t * D, D)]
                        nc.scalar.activation(r, r, ACT.Identity, bias=ht_shift[:, nb], scale=ht_rstd[:, nb]).then_inc(centred, 1)

                def context_T(k):
                    for c in range(DC):
                        act.wait_ge(tp_ready2, DC * k + c + 2)
                        if c == 0:
                            act.wait_ge(row_ready2, TT * k + 1)
                        nc.scalar.activation(cT[:, c, :], tp[c][:, :], ACT.Copy).then_inc(cT_ready, 1)

                centre(0)
                with act.Fori(0, NTB - 1) as k:
                    centre(k + 1)
                    context_T(k)
                act.wait_ge(w1_in, 16)
                nc.scalar.activation(w1_hi[:, :, :], w1[:, :, :], ACT.Copy).then_inc(w_hi, 1)
                act.wait_ge(w2_in, 16)
                nc.scalar.activation(w2_hi[:, :, :], w2[:, :, :], ACT.Copy).then_inc(w_hi, 1)
                context_T(NTB - 1)
                act.wait_ge(var2, 1)
                nc.scalar.activation(rstd[:, :], tmp[:, 3, :], ACT.Sqrt).then_inc(std2, 1)

                def h2_high(k):
                    for c in range(DC):
                        act.wait_ge(tp_ready2, DC * (NTB + k) + c + 2)
                        if k > 0 and c == 0:
                            act.wait_ge(up_ready, FC * k)
                        nc.scalar.activation(h2_hi[:, c, :], tp[c][:, :], ACT.Copy).then_inc(h2_hi_ready, 1)

                h2_high(0)
                for k in range(NTB):
                    for f in range(FC):
                        j = FC * k + f
                        act.wait_ge(up_ready, j + 1)
                        if j >= 2:
                            act.wait_ge(g_lo_ready, j - 1)
                        nc.scalar.activation(gelu[:, f % 2, :], up[f % 2][:, :], ACT.Gelu_apprx_tanh).then_inc(gelu_ready, 1)
                        act.wait_ge(gelu_ready, j + 1 + CREDIT)
                        if k >= 2 and f == 0:
                            act.wait_ge(row_ready2, 1 + NT + TT * (k - 1))
                        nc.scalar.activation(g_hi[:, k % 2, f, :], gelu[:, f % 2, :], ACT.Copy).then_inc(g_hi_ready, 1)
                    if k + 1 < NTB:
                        h2_high(k + 1)

            @block.vector
            def _(dve):
                chain = [0]

                def link(ins):
                    chain[0] += 1
                    ins.then_inc(link_s, 1)
                    dve.wait_ge(link_s, chain[0])

                def normalize(k):
                    dve.wait_ge(cn_ready, k + 1)
                    nc.vector.reciprocal(rden[:, :], raw(k)[:, :, VW - 1]).then_inc(csum_ready, 1)
                    nc.vector.tensor_tensor(csum[:, :, :], raw(k)[:, :, 0:HD], raw(k)[:, :, HD:2 * HD], ALU.add).then_inc(csum_ready, 1)
                    dve.wait_ge(csum_ready, 2 * k + 2)
                    dve.wait_ge(tp_ready2, DC * k + 1)
                    nc.vector.tensor_tensor(cnorm[:, :, :].rearrange("p t (h d) -> p (t h) d", h=H), csum[:, :, :],
                                            rden[:, :].unsqueeze(2).to_broadcast([P, TT * H, HD]), ALU.mult).then_inc(cn_ready, 1)

                def add_rows(k):
                    dve.wait_ge(ht_ready, k + 1)
                    for t in range(TT):
                        n = k * TT + t
                        r = mask_ctx[:, bass.ds(k * BLK32 + CTX_TB + t * D, D)]
                        dve.wait_ge(row_ready2, n + 2)
                        nc.vector.tensor_tensor(r, row[t % 2][:, :], r, ALU.add).then_inc(row_read, 1)
                        dve.wait_ge(row_read, n + 1 + CREDIT)
                        nc.vector.bn_stats(stats[:, bass.ds(n, 1), :], r).then_inc(stat2, 1)

                normalize(0)
                with dve.Fori(0, NTB - 1) as k:
                    normalize(k + 1)
                    add_rows(k)
                add_rows(NTB - 1)
                dve.wait_ge(stat2, NT)
                me, qe, mo, qo = (stats[:, :, i] for i in (1, 2, 4, 5))
                link(nc.vector.tensor_tensor(tmp[:, 0, :], me, mo, ALU.subtract))
                link(nc.vector.tensor_tensor(tmp[:, 1, :], qe, qo, ALU.add))
                link(nc.vector.tensor_tensor(tmp[:, 2, :], me, mo, ALU.add))
                link(nc.vector.tensor_scalar(mean[:, :], tmp[:, 2, :], 0.5, None, ALU.mult))
                link(nc.vector.tensor_tensor(tmp[:, 0, :], tmp[:, 0, :], tmp[:, 0, :], ALU.mult))
                link(nc.vector.scalar_tensor_tensor(out=tmp[:, 1, :], in0=tmp[:, 0, :], scalar=D / 4.0,
                                                    in1=tmp[:, 1, :], op0=ALU.mult, op1=ALU.add))
                nc.vector.tensor_scalar(tmp[:, 3, :], tmp[:, 1, :], 1.0 / D, EPS, ALU.mult, ALU.add).then_inc(var2, 1)
                dve.wait_ge(std2, 1)
                link(nc.vector.reciprocal(rstd[:, :], rstd[:, :]))
                link(nc.vector.tensor_tensor(rstd[:, :], rstd[:, :], node_f[:, :], ALU.mult))

                def second_norm(k):
                    r = res(k)
                    for t in range(TT):
                        n = k * TT + t
                        last = nc.vector.tensor_scalar(r[:, t, :], r[:, t, :], mean[:, n:n + 1], rstd[:, n:n + 1],
                                                       ALU.subtract, ALU.mult)
                    link(last)
                    link(nc.vector.tensor_tensor(r, r, vecs[:, LN2_G, :].unsqueeze(1).to_broadcast([P, TT, D]), ALU.mult))
                    if k > 0:
                        dve.wait_ge(tp_ready2, 1 + DC * (k + NTB))
                        dve.wait_ge(res_ready, k)
                    for t in range(TT):
                        n = k * TT + t
                        last = nc.vector.scalar_tensor_tensor(out=h2[:, t, :], in0=vecs[:, LN2_B, :], scalar=node_f[:, n:n + 1],
                                                              in1=r[:, t, :], op0=ALU.mult, op1=ALU.add)
                    last.then_inc(h2_ready, 1)

                def h2_low(k):
                    for c in range(DC):
                        dve.wait_ge(h2_hi_ready, DC * k + c + 1)
                        nc.vector.tensor_tensor(h2_lo[:, c, :], tp[c][:, :], h2_hi[:, c, :], ALU.subtract).then_inc(h2_lo_ready, 1)

                def store_rows(k):
                    dve.wait_ge(res_ready, k + 1)
                    for t in range(TT):
                        b, n = t % 2, k * TT + t
                        i = n // 2
                        dve.wait_ge(row_ready2, NT + n + 2)
                        if i > 0:
                            dve.wait_ge(stored[b], 16 * i)
                        nc.vector.tensor_tensor(yout[b][:, :], row[b][:, :], xin[:, n, :], ALU.add).then_inc(y_out, 1)

                second_norm(0)
                h2_low(0)
                for k in range(NTB):
                    if k + 1 < NTB:
                        second_norm(k + 1)
                    for f in range(FC):
                        dve.wait_ge(g_hi_ready, FC * k + f + 1)
                        nc.vector.tensor_tensor(g_lo[:, k % 2, f, :], gelu[:, f % 2, :], g_hi[:, k % 2, f, :],
                                                ALU.subtract).then_inc(g_lo_ready, 1)
                    if k + 1 < NTB:
                        h2_low(k + 1)
                    if k > 0:
                        store_rows(k - 1)
                store_rows(NTB - 1)

            @block.tensor
            def _(pe):
                for s in (row_read, y_out, gelu_ready):
                    pe.sem_inc(s, CREDIT)
                for s in (cn_ready, tp_ready2, cT_ready, row_ready2):
                    pe.sem_inc(s, 1)

                def turn(tile):
                    for c in range(DC):
                        for t in range(TT):
                            last = nc.tensor.transpose(tp[c][:, t * P:(t + 1) * P], tile(t, c), ident32[:, :])
                        last.then_inc(tp_ready2, 1)

                def turn_context(k):
                    pe.wait_ge(cn_ready, k + 2)
                    pe.wait_ge(cT_ready, DC * k + 1)
                    turn(lambda t, c: cnorm[:, t, c * P:(c + 1) * P])

                def project(k):
                    pe.wait_ge(cT_ready, DC * (k + 1) + 1)
                    for t in range(TT):
                        pe.wait_ge(row_read, k * TT + t + 1)
                        for c in range(DC):
                            last = nc.tensor.matmul(row[t % 2][:, :], cT[:, c, t * P:(t + 1) * P], wo[:, c, :],
                                                    start=(c == 0), stop=(c == DC - 1))
                        last.then_inc(row_ready2, 1)

                turn_context(0)
                with pe.Fori(0, NTB - 1) as k:
                    project(k)
                    turn_context(k + 1)
                project(NTB - 1)
                pe.wait_ge(row_read, NT + CREDIT)

                def turn_block(k):
                    pe.wait_ge(h2_ready, k + 1)
                    if k > 0:
                        pe.wait_ge(h2_lo_ready, DC * k)
                    turn(lambda t, c: h2[:, t, c * P:(c + 1) * P])

                def up_products(k):
                    pe.wait_ge(h2_lo_ready, DC * (k + 1))
                    if k == 0:
                        pe.wait_ge(w1_split, 1)
                    for f in range(FC):
                        pe.wait_ge(gelu_ready, FC * k + f + 1)
                        terms = [(w, h, c) for c in range(DC) for w, h in ((w1_hi, h2_hi), (w1_lo, h2_hi), (w1_hi, h2_lo))]
                        for i, (w, h, c) in enumerate(terms):
                            last = nc.tensor.matmul(up[f % 2][:, :], w[:, c, f * P:(f + 1) * P], h[:, c, :],
                                                    start=(i == 0), stop=(i == len(terms) - 1))
                        last.then_inc(up_ready, 1)

                def down_products(k):
                    pe.wait_ge(g_lo_ready, FC * (k + 1))
                    if k == 0:
                        pe.wait_ge(w2_split, 1)
                    for t in range(TT):
                        pe.wait_ge(y_out, k * TT + t + 1)
                        cols = slice(t * P, (t + 1) * P)
                        terms = [(a, w, f) for f in range(FC) for a, w in ((g_hi, w2_hi), (g_hi, w2_lo), (g_lo, w2_hi))]
                        for i, (a, w, f) in enumerate(terms):
                            last = nc.tensor.matmul(row[t % 2][:, :], a[:, k % 2, f, cols], w[:, f, :],
                                                    start=(i == 0), stop=(i == len(terms) - 1))
                        last.then_inc(row_ready2, 1)

                turn_block(0)
                for k in range(NTB):
                    up_products(k)
                    if k + 1 < NTB:
                        turn_block(k + 1)
                    if k > 0:
                        down_products(k - 1)
                down_products(NTB - 1)


_INS = ["x", "adj", "nodemask", "L0_gnn_h_target", "L0_gnn_ln1_scale", "L0_gnn_ln1_bias", "L0_gnn_Wq", "L0_gnn_bq",
        "L0_gnn_Wk", "L0_gnn_bk", "L0_gnn_Wv", "L0_gnn_bv", "L0_gnn_Wo", "L0_gnn_bo", "L0_gnn_ln2_scale",
        "L0_gnn_ln2_bias", "L0_gnn_W1", "L0_gnn_W2"]


def kernel(**inputs):
    import numpy as np
    import concourse.bacc as bacc
    from concourse import mybir as mb
    from concourse.bass_utils import run_bass_kernel_spmd

    nc = bacc.Bacc("TRN2", target_bir_lowering=False, num_devices=1)
    arrays, args = {}, []
    for name in _INS:
        a = np.ascontiguousarray(inputs[name])
        arrays[f"in_{name}"] = a
        args.append(nc.dram_tensor(f"in_{name}", a.shape, mb.dt.from_np(a.dtype), kind="ExternalInput").ap())
    out = nc.dram_tensor("out_y", (N, D), mb.dt.from_np(np.dtype("float32")), kind="ExternalOutput").ap()
    gnn_kernel(nc, *args, out)
    r = run_bass_kernel_spmd(nc, [arrays], core_ids=[0])
    return r.results[0]["out_y"]
```

```python
from contextlib import ExitStack

import concourse.bass as bass
from concourse import mybir

F32 = mybir.dt.float32
F16 = mybir.dt.float16
BF16 = mybir.dt.bfloat16
I32 = mybir.dt.int32
ALU = mybir.AluOpType
ACT = mybir.ActivationFunctionType

P = 128
N = 2048
D = 256
H = 8
HD = D // H
F = 4 * D
NT = N // P
DC = D // P
FC = F // P
TB = 512
TT = TB // P
NTB = N // TB
UNITS = NTB * H
STEPS = NT
PAIRS = STEPS // 2
AHEAD = 3
SHIFT_ROW = 3 * HD
VW = 2 * HD + 1
VS = VW + 1
CTX_TB = TT * H * VW
BLK32 = TT * N // 2
NEG = -1e30
EPS = 1e-5
INV_SQRT_HD = float(HD) ** -0.5
SHIFT_MAX = 60000.0
NORM_AT = (NTB - 1) * BLK32 + CTX_TB + TT * D
CREDIT = 2
CTX0 = 2176
assert CTX0 >= CTX_TB and BLK32 >= CTX_TB + TT * D and CTX0 % 2 == 0
assert NORM_AT + (NTB - 1) * TT * D <= CTX0 + NTB * BLK32


def bcast_rows(vec):
    return vec.partition_broadcast(P)


def gnn_kernel(nc, x, adj, nodemask, h_target, ln1_scale, ln1_bias, Wq, bq, Wk, bk, Wv, bv, Wo, bo,
               ln2_scale, ln2_bias, W1, W2, out):
    with ExitStack() as top:
        def sb(stack, name, shape, dt):
            return stack.enter_context(nc.sbuf_tensor(name, shape, dt))

        def psum(stack, name, shape, dt=F32):
            return stack.enter_context(nc.psum_tensor(name, shape, dt))

        def sem(name):
            return top.enter_context(nc.semaphore(name))

        mask_ctx = sb(top, "mask_ctx", [P, CTX0 + NTB * BLK32], F32)
        mask_nat = mask_ctx[:, CTX0:].bitcast(BF16).rearrange("p (t s) -> p t s", s=N)
        node_f = sb(top, "node_f", [P, NT], F32)
        rstd = sb(top, "rstd", [P, 2 * NT], F32)
        nshift = sb(top, "nshift", [P, 2 * NT], F32)
        rden = sb(top, "rden", [P, NTB, TT * H], F32)
        ident32 = sb(top, "ident32", [P, P], F32)
        ident16 = sb(top, "ident16", [P, P], F16)
        identb = sb(top, "identb", [P, P], BF16)

        weights = sb(top, "weights", [P, (DC + 5) * D], F32)
        wo = weights[:, :DC * D].rearrange("p (c d) -> p c d", c=DC)
        vecs = weights[:, DC * D:].rearrange("p (k d) -> p k d", k=5)

        attn_mem = ExitStack()
        kT = sb(attn_mem, "kT", [P, H, N], F16)
        qT = sb(attn_mem, "qT", [P, UNITS, TB], F16)
        v_sb = sb(attn_mem, "v_sb", [P, NT, H, VS], F16)

        prologue(nc, sb, psum, sem, locals())
        attention(nc, sb, psum, sem, locals())
        attn_mem.close()
        epilogue(nc, sb, psum, sem, locals())


def raw_context(mask_ctx, k):
    return mask_ctx[:, k * BLK32:k * BLK32 + CTX_TB].rearrange("p (a w) -> p a w", w=VW)


def normed_context(mask_ctx, k):
    return mask_ctx[:, NORM_AT + k * TT * D:NORM_AT + (k + 1) * TT * D].rearrange("p (t d) -> p t d", t=TT)


def prologue(nc, sb, psum, sem, g):
    x, adj, nodemask, h_target = g["x"], g["adj"], g["nodemask"], g["h_target"]
    kT, qT, v_sb, mask_nat, node_f = g["kT"], g["qT"], g["v_sb"], g["mask_nat"], g["node_f"]
    ident32, ident16, identb = g["ident32"], g["ident16"], g["identb"]
    rstd, nshift = g["rstd"], g["nshift"]
    with ExitStack() as mem:
        src = qT[:, UNITS // 2:, :].bitcast(F32).rearrange("p u t -> p (u t)").rearrange("p (t d) -> p t d", d=D)
        tgt = sb(mem, "tgt", [P, NT, D], F32)
        adj_in = sb(mem, "adj_in", [P, 2, N], I32)
        wkv = g["weights"][:, :2 * DC * D].rearrange("p (c k d) -> p c k d", c=DC, k=2)
        wq = g["weights"][:, 2 * DC * D:3 * DC * D].rearrange("p (c d) -> p c d", c=DC)
        spare = g["mask_ctx"]
        bias_kv = spare[:, 0:2 * D].rearrange("p (k d) -> p k d", k=2)
        bias_q = spare[:, 2 * D:3 * D]
        normed = [spare[:, (3 + i) * D:(4 + i) * D] for i in range(2)]
        assert 5 * D <= CTX0
        ln1_g = sb(mem, "ln1_g", [P, DC], F32)
        ln1_b = sb(mem, "ln1_b", [P, DC], F32)
        node_i = sb(mem, "node_i", [P, NT], I32)
        nT = [sb(mem, f"nT{i}", [P, DC, P], F32) for i in range(2)]
        kvf = [sb(mem, f"kvf{i}", [P, 2, D], F32) for i in range(2)]
        stack = [sb(mem, f"stack{i}", [P, H, P], F16) for i in range(2)]
        stats = sb(mem, "stats", [P, 2 * NT, 6], F32)
        tmp = sb(mem, "tmp", [P, 4, 2 * NT], F32)
        mean = sb(mem, "mean", [P, 2 * NT], F32)
        deg_half = sb(mem, "deg_half", [P, NT, 2], F32)
        deg = sb(mem, "deg", [P, NT], F32)
        q_scale = sb(mem, "q_scale", [P, NT], F32)
        neg_big = sb(mem, "neg_big", [P, NT], F32)

        tpose = [psum(mem, f"tpose{i}", [P, DC, P]) for i in range(2)]
        proj = [psum(mem, f"proj{i}", [P, 2, D]) for i in range(2)]
        stackT = [psum(mem, f"stackT{i}", [P, H, P], F16) for i in range(2)]

        WEIGHTS = 9 * 16
        src_in, tgt_in = ([sem(f"{w}_in{i}") for i in range(NTB)] for w in ("src", "tgt"))
        wts_in, adj_here = sem("wts_in"), [sem(f"adj_here{h}") for h in range(2)]
        ident_made = sem("ident_made")
        stat_done, fin, var_ready, std_ready, rstd_ready = (
            sem("stat_done"), sem("fin"), sem("var_ready"), sem("std_ready"), sem("rstd_ready"))
        relu_done, norm_done = sem("relu_done"), sem("norm_done")
        tp_ready, nT_ready, proj_ready = sem("tp_ready"), sem("nT_ready"), sem("proj_ready")
        kv_ready, hi_ready, stack_ready, v_lo = sem("kv_ready"), sem("hi_ready"), sem("stack_ready"), sem("v_lo")
        stT_ready, stT_done = sem("stT_ready"), sem("stT_done")
        deg_ready, deg_sum, scale_ready, big_ready, mask_done = sem("deg_ready"), sem("deg_sum"), sem("scale_ready"), sem("big_ready"), sem("mask_done")
        k_ready, v_hi = sem("k_ready"), sem("v_hi")

        def heads(row):
            return row.rearrange("p (h d) -> p h d", h=H)

        def v_tile(n):
            return v_sb[:, bass.ds(n, 1), :, :].rearrange("p t h w -> p (t h) w")

        def mask_half(m, h):
            return mask_nat[:, bass.ds(m, 1), h * N // 2:(h + 1) * N // 2].rearrange("p t s -> p (t s)")

        def adj_half(m, h):
            return adj_in[:, bass.ds(m % 2, 1), h * N // 2:(h + 1) * N // 2].rearrange("p o s -> p (o s)")

        with nc.Block() as block:
            @block.sync
            def _(sp):
                for rows, dst, here in ((x, src, src_in), (h_target, tgt, tgt_in)):
                    for c in range(NTB):
                        sp.dma_start(dst[:, c * TT:(c + 1) * TT, :],
                                     rows[c * TB:(c + 1) * TB, :].rearrange("(t p) d -> p t d", p=P)).then_inc(here[c], 16)
                for i, w in enumerate((g["Wk"], g["Wv"])):
                    sp.dma_start(wkv[:, :, i, :], w.rearrange("(c p) n -> p c n", p=P)).then_inc(wts_in, 16)
                sp.dma_start(wq[:, :, :], g["Wq"].rearrange("(c p) n -> p c n", p=P)).then_inc(wts_in, 16)
                for i, b in enumerate((g["bk"], g["bv"])):
                    sp.dma_start(bias_kv[:, i, :], bcast_rows(b)).then_inc(wts_in, 16)
                sp.dma_start(bias_q[:, :], bcast_rows(g["bq"])).then_inc(wts_in, 16)
                with nc.allow_non_contiguous_dma(reason="small vectors, one element per partition"):
                    sp.dma_start(ln1_g[:, :], g["ln1_scale"].rearrange("(c p) -> p c", p=P)).then_inc(wts_in, 16)
                    sp.dma_start(ln1_b[:, :], g["ln1_bias"].rearrange("(c p) -> p c", p=P)).then_inc(wts_in, 16)
                    sp.dma_start(node_i[:, :], nodemask.rearrange("(t p) -> p t", p=P)).then_inc(wts_in, 16)
                with sp.Fori(0, NT) as m:
                    for h in range(2):
                        sp.wait_ge(mask_done, 2 * m + h + 1)
                        sp.wait_ge(adj_here[h], 16 * m + 1)
                        sp.dma_start(adj_half(m, h), adj[bass.ds(m * P, P), h * N // 2:(h + 1) * N // 2]).then_inc(adj_here[h], 16)

            @block.gpsimd
            def _(pool):
                for m in (ident32, ident16, identb):
                    nc.gpsimd.memset(m[:, :], 0.0).then_inc(ident_made, 1)
                pool.wait_ge(ident_made, 3)
                for m in (ident32, ident16, identb):
                    nc.gpsimd.affine_select(out=m[:, :], in_=m[:, :], compare_op=ALU.not_equal, fill=1.0, base=0,
                                            pattern=[[-1, P]], channel_multiplier=1).then_inc(ident_made, 1)
                for s in stack:
                    nc.gpsimd.memset(s[:, :, :], 0.0).then_inc(ident_made, 1)
                pool.wait_ge(ident_made, 8)
                for s in stack:
                    nc.gpsimd.memset(s[:, :, SHIFT_ROW:SHIFT_ROW + 1], 1.0).then_inc(ident_made, 1)
                nc.gpsimd.memset(v_sb[:, :, :, 2 * HD:VS], 1.0).then_inc(ident_made, 1)

                def low_part(n, b, at):
                    pool.wait_ge(hi_ready, n + 1)
                    nc.gpsimd.tensor_tensor(stack[b][:, :, at * HD:(at + 1) * HD], heads(kvf[b][:, 0, :]),
                                            stack[b][:, :, 0:HD], ALU.subtract).then_inc(stack_ready, 1)

                with pool.Fori(0, NT // 2) as i:
                    for b in range(2):
                        low_part(2 * i + b, b, 2)
                        pool.wait_ge(v_hi, 2 * i + b + 1)
                        nc.gpsimd.tensor_tensor(v_tile(2 * i + b)[:, :, HD:2 * HD], heads(kvf[b][:, 1, :]),
                                                v_tile(2 * i + b)[:, :, 0:HD], ALU.subtract).then_inc(v_lo, 1)
                for b in range(2):
                    pool.wait_ge(hi_ready, NT + b + 1)
                    nc.gpsimd.memset(stack[b][:, :, SHIFT_ROW:SHIFT_ROW + 1], 0.0).then_inc(ident_made, 1)
                    pool.wait_ge(ident_made, 12 + b)
                    low_part(NT + b, b, 1)
                with pool.Fori(NT // 2 + 1, NT) as i:
                    for b in range(2):
                        low_part(2 * i + b, b, 1)

            @block.scalar
            def _(act):
                act.wait_ge(var_ready, 1)
                nc.scalar.activation(rstd[:, 0:NT], tmp[:, 3, 0:NT], ACT.Sqrt).then_inc(std_ready, 1)
                act.wait_ge(rstd_ready, 1)
                with act.Fori(0, NTB) as i:
                    for t in range(TT):
                        nb = bass.ds(i * TT + t, 1)
                        nc.scalar.activation(src[:, nb, :], src[:, nb, :], ACT.Relu, bias=nshift[:, nb],
                                             scale=rstd[:, nb]).then_inc(relu_done, 1)
                act.wait_ge(var_ready, 2)
                nc.scalar.activation(rstd[:, :], tmp[:, 3, :], ACT.Sqrt).then_inc(std_ready, 1)

                def features(n, b):
                    act.wait_ge(tp_ready, n + 1 + CREDIT)
                    act.wait_ge(proj_ready, n + 1)
                    for c in range(DC):
                        last = nc.scalar.activation(nT[b][:, c, :], tpose[b][:, c, :], ACT.Identity,
                                                    bias=ln1_b[:, c:c + 1], scale=ln1_g[:, c:c + 1])
                    last.then_inc(nT_ready, 1)

                def high_parts(n, b, kind):
                    act.wait_ge(k_ready, n + 1)
                    act.wait_ge(stT_ready, n + 1)
                    kq = heads(kvf[b][:, 0, :]).unsqueeze(2).to_broadcast([P, H, 2, HD])
                    st = stack[b][:, :, :].rearrange("p h (r d) -> p h r d", r=4)
                    if kind == "target":
                        nc.scalar.activation(st[:, :, 0:3:2, :], kq, ACT.Copy).then_inc(hi_ready, 1)
                        return
                    nc.scalar.activation(st[:, :, 0:2, :], kq, ACT.Copy).then_inc(hi_ready, 1)
                    act.wait_ge(kv_ready, n + 1 + CREDIT)
                    nc.scalar.activation(v_tile(n)[:, :, 0:HD], heads(kvf[b][:, 1, :]), ACT.Copy).then_inc(v_hi, 1)

                def degrees(m, h):
                    act.wait_ge(adj_here[h], 16 * (m + 1) + 1)
                    nc.scalar.activation(mask_half(m, h), adj_half(m, h), ACT.Square,
                                         accum_out=deg_half[:, bass.ds(m, 1), h]).then_inc(deg_ready, 1)

                def pair(i, kind, last=False):
                    for b in range(2):
                        if not last or b == 0:
                            features(2 * i + b + 1, 1 - b)
                        high_parts(2 * i + b, b, kind)
                        if not last:
                            degrees(i + 1, b)

                act.wait_ge(wts_in, WEIGHTS)
                features(0, 0)
                for h in range(2):
                    degrees(0, h)
                with act.Fori(0, NT // 2) as i:
                    pair(i, "source")
                with act.Fori(NT // 2, NT - 1) as i:
                    pair(i, "target")
                pair(NT - 1, "target", True)

            @block.vector
            def _(dve):
                chain = [0]

                def link(ins):
                    chain[0] += 1
                    ins.then_inc(fin, 1)
                    dve.wait_ge(fin, chain[0])

                def count_in(tiles, c, first):
                    for t in range(c * TT, (c + 1) * TT):
                        nc.vector.bn_stats(stats[:, first + t, :], tiles[:, t, :]).then_inc(stat_done, 1)

                def spread(cols, done):
                    dve.wait_ge(stat_done, done)
                    me, qe, mo, qo = (stats[:, cols, k] for k in (1, 2, 4, 5))
                    t0, t1, t2, t3 = (tmp[:, k, cols] for k in range(4))
                    link(nc.vector.tensor_tensor(t0, me, mo, ALU.subtract))
                    link(nc.vector.tensor_tensor(t1, qe, qo, ALU.add))
                    link(nc.vector.tensor_tensor(t2, me, mo, ALU.add))
                    link(nc.vector.tensor_scalar(mean[:, cols], t2, 0.5, None, ALU.mult))
                    link(nc.vector.tensor_tensor(t0, t0, t0, ALU.mult))
                    link(nc.vector.scalar_tensor_tensor(out=t1, in0=t0, scalar=D / 4.0, in1=t1, op0=ALU.mult, op1=ALU.add))
                    nc.vector.tensor_scalar(t3, t1, 1.0 / D, EPS, ALU.mult, ALU.add).then_inc(var_ready, 1)

                def invert(cols, done):
                    dve.wait_ge(std_ready, done)
                    link(nc.vector.reciprocal(rstd[:, cols], rstd[:, cols]))
                    nc.vector.scalar_tensor_tensor(out=nshift[:, cols], in0=mean[:, cols], scalar=-1.0, in1=rstd[:, cols],
                                                   op0=ALU.mult, op1=ALU.mult).then_inc(rstd_ready, 1)

                def normalize(n, b, tiles):
                    m = n if tiles is src else n - NT
                    dve.wait_ge(tp_ready, n + 1)
                    nc.vector.tensor_scalar(normed[b][:, :], tiles[:, bass.ds(m, 1), :].rearrange("p t d -> p (t d)"),
                                            mean[:, bass.ds(n, 1)], rstd[:, bass.ds(n, 1)],
                                            ALU.subtract, ALU.mult).then_inc(norm_done, 1)

                dve.sem_inc(mask_done, 2 * CREDIT)
                sources, both = slice(0, NT), slice(0, 2 * NT)
                for c in range(NTB):
                    dve.wait_ge(src_in[c], 16)
                    count_in(src, c, 0)
                spread(sources, NT)
                invert(sources, 1)
                for c in range(NTB):
                    dve.wait_ge(tgt_in[c], 16)
                    count_in(tgt, c, NT)
                    dve.wait_ge(relu_done, (c + 1) * TT)
                    count_in(src, c, 0)
                spread(both, 3 * NT)
                dve.wait_ge(wts_in, WEIGHTS)
                link(nc.vector.tensor_scalar(node_f[:, :], node_i[:, :], 1.0, None, ALU.is_equal))
                invert(both, 2)

                def project(n, b, kind):
                    dve.wait_ge(proj_ready, n + 1 + CREDIT)
                    dve.wait_ge(stack_ready, n + 1)
                    if kind == "source":
                        dve.wait_ge(v_lo, n + 1)
                        for k, done in enumerate((k_ready, kv_ready)):
                            nc.vector.scalar_tensor_tensor(
                                out=kvf[b][:, k, :], in0=proj[b][:, k, :], scalar=node_f[:, bass.ds(n, 1)],
                                in1=bias_kv[:, k, :], op0=ALU.mult, op1=ALU.add).then_inc(done, 1)
                        return
                    m = n - NT
                    dve.wait_ge(v_lo, NT + CREDIT)
                    nc.vector.scalar_tensor_tensor(out=kvf[b][:, 1, :], in0=proj[b][:, 0, :],
                                                   scalar=node_f[:, bass.ds(m, 1)], in1=bias_q[:, :],
                                                   op0=ALU.mult, op1=ALU.add).then_inc(kv_ready, 1)
                    dve.wait_ge(kv_ready, n + 1 + CREDIT)
                    dve.wait_ge(scale_ready, m + 1)
                    nc.vector.tensor_scalar(kvf[b][:, 0, :], kvf[b][:, 1, :], q_scale[:, bass.ds(m, 1)], None,
                                            ALU.mult).then_inc(k_ready, 1)

                def edge_scales(m):
                    nb = bass.ds(m, 1)
                    dve.wait_ge(deg_ready, 2 * m + 2)
                    nc.vector.tensor_tensor(deg[:, nb], deg_half[:, nb, 0], deg_half[:, nb, 1], ALU.add).then_inc(deg_sum, 1)
                    dve.wait_ge(deg_sum, m + 1)
                    nc.vector.tensor_scalar(q_scale[:, nb], deg[:, nb], 0.0, INV_SQRT_HD, ALU.is_gt, ALU.mult).then_inc(scale_ready, 1)
                    nc.vector.tensor_scalar(neg_big[:, nb], deg[:, nb], 0.0, NEG, ALU.is_gt, ALU.mult).then_inc(big_ready, 1)

                def make_mask(m, h):
                    dve.wait_ge(big_ready, m + 1)
                    nc.vector.tensor_scalar(mask_half(m, h), adj_half(m, h), 0.0, neg_big[:, bass.ds(m, 1)],
                                            ALU.is_equal, ALU.mult).then_inc(mask_done, 1)

                def stack_out(n, b, dst):
                    dve.wait_ge(stT_ready, n + 1 + CREDIT)
                    nc.vector.tensor_copy(dst, stackT[b][:, :, :]).then_inc(stT_done, 1)

                def k_place(n):
                    return kT[:, :, bass.ds(n * P, P)]

                def q_place(i, t):
                    return qT[:, bass.ds(i * H, H), t * P:(t + 1) * P]

                def tile(n, i, b, kind, ahead, before):
                    if ahead is not None:
                        normalize(n + 2, b, ahead)
                    if b == 0:
                        edge_scales(i)
                    project(n, b, kind)
                    if before is not None:
                        stack_out(n - 1, 1 - b, before)
                    make_mask(i, b)

                def source_pair(i, ahead):
                    for b in range(2):
                        n = 2 * i + b
                        tile(n, i, b, "source", ahead, k_place(n - 1))

                for n in range(2):
                    normalize(n, n, src)
                tile(0, 0, 0, "source", src, None)
                tile(1, 0, 1, "source", src, k_place(0))
                with dve.Fori(1, NT // 2 - 1) as i:
                    source_pair(i, src)
                source_pair(NT // 2 - 1, tgt)

                def target_block(blk, first, ahead=TT):
                    for t in range(TT):
                        n = blk * TT + t + NT
                        tile(n, blk * (TT // 2) + t // 2 + NT // 2, t % 2, "target", tgt if t < ahead else None,
                             first if t == 0 else q_place(blk, t - 1))

                target_block(0, k_place(NT - 1))
                with dve.Fori(1, NTB - 1) as blk:
                    target_block(blk, q_place(blk - 1, TT - 1))
                target_block(NTB - 1, q_place(NTB - 2, TT - 1), TT - 2)
                stack_out(2 * NT - 1, 1, q_place(NTB - 1, TT - 1))
                dve.wait_ge(stT_done, 2 * NT + CREDIT)

            @block.tensor
            def _(pe):
                for s in (nT_ready, proj_ready, kv_ready, stack_ready, stT_ready, stT_done, v_lo, tp_ready):
                    pe.sem_inc(s, CREDIT)
                for s in adj_here:
                    pe.sem_inc(s, 1)
                pe.wait_ge(ident_made, 11)
                pe.wait_ge(wts_in, WEIGHTS)
                wkv_c = wkv[:, :, :, :].rearrange("p c k d -> p c (k d)")

                def turn(n, b):
                    pe.wait_ge(norm_done, n + 1)
                    pe.wait_ge(nT_ready, n + 1)
                    for c in range(DC):
                        last = nc.tensor.transpose(tpose[b][:, c, :], normed[b][:, c * P:(c + 1) * P], ident32[:, :])
                    last.then_inc(tp_ready, 1)

                def project(n, b, w, width):
                    pe.wait_ge(nT_ready, n + 1 + CREDIT)
                    pe.wait_ge(kv_ready, n + 1)
                    for c in range(DC):
                        last = nc.tensor.matmul(proj[b][:, 0:width, :].rearrange("p k d -> p (k d)"), nT[b][:, c, :],
                                                w[:, c, :], start=(c == 0), stop=(c == DC - 1))
                    last.then_inc(proj_ready, 1)

                def turn_stack(n, b):
                    pe.wait_ge(stack_ready, n + 1 + CREDIT)
                    pe.wait_ge(stT_done, n + 1)
                    for h in range(H):
                        last = nc.tensor.transpose(stackT[b][:, h, :], stack[b][:, h, :], ident16[:, :])
                    last.then_inc(stT_ready, 1)

                def step(n, b, w, width, first=False, ahead=True):
                    if ahead:
                        turn(n + 1, 1 - b)
                    project(n, b, w, width)
                    if not first:
                        turn_stack(n - 1, 1 - b)

                kv, q = (wkv_c, 2), (wq[:, :, :], 1)
                turn(0, 0)
                step(0, 0, *kv, first=True)
                step(1, 1, *kv)
                with pe.Fori(1, NT // 2) as i:
                    for b in range(2):
                        step(2 * i + b, b, *kv)
                with pe.Fori(NT // 2, NT - 1) as i:
                    for b in range(2):
                        step(2 * i + b, b, *q)
                for b in range(2):
                    step(2 * NT - 2 + b, b, *q, ahead=b == 0)
                turn_stack(2 * NT - 1, 1)


def attention(nc, sb, psum, sem, g):
    kT, qT, v_sb, mask_nat, mask_ctx = g["kT"], g["qT"], g["v_sb"], g["mask_nat"], g["mask_ctx"]
    ident16, identb = g["ident16"], g["identb"]
    SLOTS = 4
    MASK_UNITS = UNITS - H
    PER_UNIT = NT // H
    LEAD = 2
    with ExitStack() as mem:
        mask_T = sb(mem, "mask_T", [P, 2, NT, TB], BF16)
        prob = sb(mem, "prob", [P, SLOTS, TB], F32)
        prob_lo = sb(mem, "prob_lo", [P, SLOTS, TB], F16)
        masked = g["weights"][:, DC * D:DC * D + N // 2].bitcast(BF16).rearrange("p (i s) -> p i s", i=2)
        half_max = sb(mem, "half_max", [P, PAIRS], F32)
        row_max = sb(mem, "row_max", [P, TT], F32)
        shift = sb(mem, "shift", [P, TT, SHIFT_ROW + 1], F16)
        score = [psum(mem, f"score{i}", [P, TB]) for i in range(2)]
        early = [psum(mem, f"early{i}", [P, N // 2]) for i in range(2)]
        ctx = psum(mem, "ctx", [P, TT, VW])
        turned = psum(mem, "turned", [P, TB])
        turned_b = turned[:, :].bitcast(BF16)[:, 0:TB]
        first_b = [score[i][:, :].bitcast(BF16)[:, 0:TB] for i in range(2)]

        score_ready = sem("score_ready")
        exp_done = sem("exp_done")
        lo_even, lo_odd = sem("lo_even"), sem("lo_odd")
        ctx_done = sem("ctx_done")
        ctx_out = sem("ctx_out")
        early_ready = sem("early_ready")
        max_done = sem("max_done")
        small = sem("small")
        shift_zero, shift_ready = sem("shift_zero"), sem("shift_ready")
        row_ready, row_done = sem("row_ready"), sem("row_done")
        norm_step = sem("norm_step")
        next_in = sem("next_in")
        mT_ready, mT_done = sem("mT_ready"), sem("mT_done")

        def prob_hi(slot):
            return prob[:, slot, :].bitcast(BF16).rearrange("p (t two) -> p t two", two=2)[:, :, 1]

        def every_unit(eng, unit):
            with eng.Fori(0, MASK_UNITS) as u:
                unit(u, True, True, True)
            with eng.Fori(MASK_UNITS, UNITS - LEAD) as u:
                unit(u, False, True, True)
            unit(UNITS - 2, False, False, True)
            unit(UNITS - 1, False, False, False)

        with nc.Block() as block:
            @block.sync
            def _(sp):
                sp.dma_start(g["wo"][:, :, :], g["Wo"].rearrange("(c p) n -> p c n", p=P)).then_inc(next_in, 16)
                sp.wait_ge(max_done, UNITS * PAIRS + 2)
                for i, v in enumerate(("ln1_scale", "ln1_bias", "bo", "ln2_scale", "ln2_bias")):
                    sp.dma_start(g["vecs"][:, i, :], bcast_rows(g[v])).then_inc(next_in, 16)
                for k in range(NTB):
                    at = k * BLK32 + CTX_TB
                    sp.dma_start(mask_ctx[:, at:at + TT * D].rearrange("p (t d) -> p t d", d=D),
                                 g["h_target"][k * TB:(k + 1) * TB, :].rearrange("(t p) d -> p t d", p=P)).then_inc(next_in, 16)
                sp.wait_ge(next_in, (6 + NTB) * 16)

            @block.tensor
            def _(pe):
                pe.sem_inc(ctx_done, SLOTS)

                def scores(u, m, at=None):
                    n = u * STEPS + m
                    if m == 0:
                        pe.wait_ge(row_done, u + 1)
                    pe.wait_ge(exp_done, n + 1)
                    nc.tensor.matmul(score[m % 2][:, :], kT[:, bass.ds(u % H, 1), m * P:(m + 1) * P],
                                     qT[:, bass.ds(u, 1), :], start=True, stop=False)
                    nc.tensor.matmul(score[m % 2][:, :], identb[:, :], mask_T[:, bass.ds((u // H) % 2, 1), m, :],
                                     start=False, stop=True).then_inc(score_ready, 1)

                def early_scores(w, s):
                    k, half = s // 2, s % 2
                    if half == 0:
                        pe.wait_ge(max_done, w * PAIRS + k + 1)
                    last = nc.tensor.matmul(early[k % 2][:, half * TB:(half + 1) * TB],
                                            qT[:, bass.ds(w, 1), (s // 4) * P:(s // 4 + 1) * P],
                                            kT[:, bass.ds(w % H, 1), (s % 4) * TB:(s % 4 + 1) * TB], start=True, stop=True)
                    if half == 1:
                        last.then_inc(early_ready, 1)

                def shift_row(w, masks):
                    pe.wait_ge(shift_ready, w + 1)
                    pe.wait_ge(mT_done, masks + 1)
                    for t in range(TT):
                        last = nc.tensor.matmul(turned[0:SHIFT_ROW + 1, t * P:(t + 1) * P], shift[:, t, :], ident16[:, :],
                                                start=True, stop=True)
                    last.then_inc(row_ready, 1)

                def turn_mask(blk, st, bank):
                    for t in range(TT):
                        last = nc.tensor.transpose(
                            bank[:, t * P:(t + 1) * P],
                            mask_nat[:, bass.ds(blk * TT + t, 1), bass.ds(st * P, P)].rearrange("p t s -> p (t s)"),
                            identb[:, :])
                    last.then_inc(mT_ready, 1)

                def context(u, m):
                    if m == 0:
                        pe.wait_ge(ctx_out, u + 1)
                    pe.wait_ge(lo_odd if m % 2 else lo_even, u * (STEPS // 2) + m // 2 + 1)
                    for t in range(TT):
                        cols = slice(t * P, (t + 1) * P)
                        v_h = v_sb[:, m, bass.ds(u % H, 1), 0:VW]
                        nc.tensor.matmul(ctx[:, t, :], prob_hi(m % SLOTS)[:, cols], v_h, start=(m == 0 and t == 0),
                                         stop=False, skip_group_check=True)
                        last = nc.tensor.matmul(ctx[:, t, :], prob_lo[:, m % SLOTS, cols], v_h, start=False,
                                                stop=(m == STEPS - 1), skip_group_check=True)
                    last.then_inc(ctx_done, 1)

                for s in range(STEPS):
                    early_scores(0, s)
                    if s >= 2:
                        pe.wait_ge(mT_done, s)
                    turn_mask(0, s, first_b[s % 2])
                shift_row(0, NT)
                for s in range(STEPS):
                    early_scores(1, s)
                for m in range(AHEAD):
                    scores(0, m)

                def unit(u, mask, early_too, more):
                    turned_before = NT + PER_UNIT * u if mask else NT * NTB
                    for s in range(STEPS):
                        if s + AHEAD < STEPS:
                            scores(u, s + AHEAD)
                        elif more:
                            scores(u + 1, s + AHEAD - STEPS)
                        if early_too:
                            for q in ([0, 1] if s == 0 else [s + 1] if s + 1 < STEPS else []):
                                early_scores(u + LEAD, q)
                        context(u, s)
                        if s == 4 and more:
                            shift_row(u + 1, turned_before)
                        if mask and s in (7, 11):
                            k = (s - 7) // 4
                            pe.wait_ge(row_done, u + 2)
                            pe.wait_ge(mT_done, turned_before + k + 1)
                            turn_mask(u // H + 1, (u % H) * PER_UNIT + k, turned_b)

                every_unit(pe, unit)

            @block.scalar
            def _(act):
                def exponential(u, m):
                    n = u * STEPS + m
                    act.wait_ge(score_ready, n + 1)
                    act.wait_ge(ctx_done, n + 1)
                    nc.scalar.activation(prob[:, m % SLOTS, :], score[m % 2][:, :], ACT.Exp).then_inc(exp_done, 1)

                def mask_out(j, buf, st, bank):
                    act.wait_ge(mT_ready, j + 1)
                    nc.scalar.activation(mask_T[:, bass.ds(buf, 1), bass.ds(st, 1), :].rearrange("p b s t -> p (b s t)"),
                                         bank, ACT.Copy).then_inc(mT_done, 1)

                def row_out(w):
                    act.wait_ge(row_ready, w + 1)
                    nc.scalar.activation(qT[SHIFT_ROW:SHIFT_ROW + 1, bass.ds(w, 1), :].rearrange("p u t -> p (u t)"),
                                         turned[SHIFT_ROW:SHIFT_ROW + 1, :], ACT.Copy).then_inc(row_done, 1)

                def context_out(u):
                    act.wait_ge(ctx_done, (u + 1) * STEPS + SLOTS)
                    dst = mask_ctx[:, bass.ds((u // H) * BLK32, CTX_TB)].rearrange("p (t h w) -> p t h w", t=TT, h=H)
                    nc.scalar.activation(dst[:, :, bass.ds(u % H, 1), :].rearrange("p t h w -> p t (h w)"), ctx[:, :, :],
                                         ACT.Copy).then_inc(ctx_out, 1)

                act.sem_inc(exp_done, 2)
                act.sem_inc(ctx_out, 1)
                act.sem_inc(mT_done, 1)
                with act.Fori(0, NT // 2) as i:
                    for b in range(2):
                        mask_out(2 * i + b, 0, 2 * i + b, first_b[b])
                row_out(0)
                for m in range(AHEAD):
                    exponential(0, m)

                def unit(u, mask, early_too, more):
                    for s in range(STEPS):
                        if s + AHEAD < STEPS:
                            exponential(u, s + AHEAD)
                        elif more:
                            exponential(u + 1, s + AHEAD - STEPS)
                        if s == 5 and more:
                            row_out(u + 1)
                        if mask and s in (8, 12):
                            k = (s - 8) // 4
                            mask_out(NT + PER_UNIT * u + k, (u // H + 1) % 2, (u % H) * PER_UNIT + k,
                                     turned_b)
                    context_out(u)

                every_unit(act, unit)

            def low_part(eng, u, m, done):
                eng.wait_ge(exp_done, u * STEPS + m + 3)
                eng.tensor_tensor(prob_lo[:, m % SLOTS, :], prob[:, m % SLOTS, :], prob_hi(m % SLOTS),
                                  ALU.subtract).then_inc(done, 1)

            @block.gpsimd
            def _(pool):
                low_part(nc.gpsimd, 0, 1, lo_odd)
                low_part(nc.gpsimd, 0, 3, lo_odd)

                def unit(u, mask, early_too, more):
                    for m in range(5, STEPS + 4, 2):
                        if m < STEPS:
                            low_part(nc.gpsimd, u, m, lo_odd)
                        elif more:
                            low_part(nc.gpsimd, u + 1, m - STEPS, lo_odd)

                every_unit(pool, unit)

            @block.vector
            def _(dve):
                def maxima(w, k, blk):
                    dve.wait_ge(early_ready, w * PAIRS + k + 1)
                    dve.wait_ge(max_done, w * PAIRS + k + 1)
                    dve.nop(nofuse=True)
                    half = slice((k % 2) * (N // 2), (k % 2 + 1) * (N // 2))
                    nc.vector.tensor_tensor_reduce(out=masked[:, k % 2, :], in0=early[k % 2][:, :],
                                                   in1=mask_nat[:, blk * TT + k // 2, half], scale=1.0, scalar=-3.0e38,
                                                   op0=ALU.add, op1=ALU.max, accum_out=half_max[:, k:k + 1]).then_inc(max_done, 1)

                def negated(w):
                    dve.wait_ge(max_done, (w + 1) * PAIRS + 2)
                    pair = half_max[:, :].rearrange("p (t two) -> p t two", two=2)
                    nc.vector.tensor_tensor(row_max[:, :], pair[:, :, 0], pair[:, :, 1], ALU.max).then_inc(small, 1)
                    dve.wait_ge(small, w + 1)
                    if not (isinstance(w, int) and w == 0):
                        dve.wait_ge(row_ready, w)
                    nc.vector.tensor_scalar(shift[:, :, SHIFT_ROW], row_max[:, :], -1.0, -SHIFT_MAX, ALU.mult,
                                            ALU.max).then_inc(shift_ready, 1)

                dve.sem_inc(max_done, 2)
                nc.vector.memset(shift[:, :, :], 0.0).then_inc(shift_zero, 1)
                dve.wait_ge(shift_zero, 1)
                for w in range(LEAD):
                    for k in range(PAIRS):
                        maxima(w, k, 0)
                    negated(w)
                for m in (0, 2):
                    low_part(nc.vector, 0, m, lo_even)

                def normalize():
                    dve.wait_ge(ctx_out, (NTB - 1) * H + 1)
                    dve.wait_ge(max_done, UNITS * PAIRS + 2)
                    for k in range(NTB - 1):
                        raw = raw_context(mask_ctx, k)
                        nc.vector.reciprocal(g["rden"][:, k, :], raw[:, :, VW - 1]).then_inc(norm_step, 1)
                        yield
                        nc.vector.tensor_tensor(raw[:, :, 0:HD], raw[:, :, 0:HD], raw[:, :, HD:2 * HD], ALU.add).then_inc(norm_step, 1)
                        yield
                        dve.wait_ge(norm_step, 3 * k + 2)
                        nc.vector.tensor_tensor(normed_context(mask_ctx, k).rearrange("p t (h d) -> p (t h) d", h=H),
                                                raw[:, :, 0:HD], g["rden"][:, k, :].unsqueeze(2).to_broadcast([P, TT * H, HD]),
                                                ALU.mult).then_inc(norm_step, 1)
                        yield

                norms = normalize()

                def unit(u, blk, more):
                    for k in range(PAIRS):
                        if blk is not None:
                            maxima(u + LEAD, k, blk)
                        m = 2 * k + 4
                        if m < STEPS:
                            low_part(nc.vector, u, m, lo_even)
                        elif more:
                            low_part(nc.vector, u + 1, m - STEPS, lo_even)
                        if blk is None:
                            next(norms, None)
                    if blk is not None:
                        negated(u + LEAD)

                for blk in range(NTB):
                    with dve.Fori(max(blk * H - LEAD, 0), (blk + 1) * H - LEAD) as u:
                        unit(u, blk, True)
                unit(UNITS - 2, None, True)
                unit(UNITS - 1, None, False)


def epilogue(nc, sb, psum, sem, g):
    mask_ctx, node_f, rden, ident32 = g["mask_ctx"], g["node_f"], g["rden"], g["ident32"]
    ht_shift, ht_rstd = g["nshift"][:, NT:], g["rstd"][:, NT:]
    wo, vecs = g["wo"], g["vecs"]
    LN1_G, LN1_B, BO, LN2_G, LN2_B = range(5)
    with ExitStack() as mem:
        xin = sb(mem, "xin", [P, NT, D], F32)
        w1 = sb(mem, "w1", [P, DC, F], F32)
        w2 = sb(mem, "w2", [P, FC, D], F32)
        w1_hi, w1_lo = (sb(mem, f"w1_{p}", [P, DC, F], F16) for p in ("hi", "lo"))
        w2_hi, w2_lo = (sb(mem, f"w2_{p}", [P, FC, D], F16) for p in ("hi", "lo"))
        csum = sb(mem, "csum", [P, TT * H, HD], F32)
        cnorm = sb(mem, "cnorm", [P, TT, D], F32)
        cT = sb(mem, "cT", [P, DC, TB], F32)
        h2 = sb(mem, "h2", [P, TT, D], F32)
        h2_hi, h2_lo = (sb(mem, f"h2_{p}", [P, DC, TB], F16) for p in ("hi", "lo"))
        gelu = sb(mem, "gelu", [P, 2, TB], F32)
        g_hi, g_lo = (sb(mem, f"g_{p}", [P, 2, FC, TB], F16) for p in ("hi", "lo"))
        yout = [sb(mem, f"yout{i}", [P, D], F32) for i in range(2)]
        stats = sb(mem, "stats2", [P, NT, 6], F32)
        tmp = sb(mem, "tmp2", [P, 4, NT], F32)
        mean = sb(mem, "mean2", [P, NT], F32)
        rstd = sb(mem, "rstd2", [P, NT], F32)
        tp = [psum(mem, f"tp{c}", [P, TB]) for c in range(DC)]
        row = [psum(mem, f"row{i}", [P, D]) for i in range(2)]
        up = [psum(mem, f"up{i}", [P, TB]) for i in range(2)]

        w1_in, w2_in, x_in = sem("w1_in"), sem("w2_in"), sem("x_in")
        link_s, bias_ready = sem("link_s"), sem("bias_ready")
        centred = sem("centred")
        scaled, ht_ready = ([sem(f"{w}{k}") for k in range(NTB)] for w in ("scaled", "ht_ready"))
        cn_ready = sem("cn_ready")
        tp_ready2, cT_ready, row_ready2, row_read = sem("tp_ready2"), sem("cT_ready"), sem("row_ready2"), sem("row_read")
        stat2, var2, std2 = sem("stat2"), sem("var2"), sem("std2")
        w_hi, w1_split, w2_split = sem("w_hi"), sem("w1_split"), sem("w2_split")
        h2_ready, res_ready = sem("h2_ready"), sem("res_ready")
        h2_hi_ready, h2_lo_ready = sem("h2_hi_ready"), sem("h2_lo_ready")
        up_ready, gelu_ready, g_hi_ready, g_lo_ready = (
            sem("up_ready"), sem("gelu_ready"), sem("g_hi_ready"), sem("g_lo_ready"))
        y_out, stored = sem("y_out"), [sem(f"stored{i}") for i in range(2)]

        def res(k):
            return mask_ctx[:, bass.ds(k * BLK32 + CTX_TB, TT * D)].rearrange("p (t d) -> p t d", d=D)

        def wide(i):
            return vecs[:, i, :].unsqueeze(1).to_broadcast([P, TT, D])

        def scale_targets(eng, k):
            eng.wait_ge(centred, TT * (k + 1))
            eng.tensor_tensor(res(k), res(k), wide(LN1_G), ALU.mult).then_inc(scaled[k], 1)
            eng.wait_ge(scaled[k], 1)
            eng.tensor_tensor(res(k), res(k), wide(LN1_B), ALU.add).then_inc(ht_ready[k], 1)

        with nc.Block() as block:
            @block.sync
            def _(sp):
                sp.dma_start(w1[:, :, :], g["W1"].rearrange("(c p) n -> p c n", p=P)).then_inc(w1_in, 16)
                sp.dma_start(w2[:, :, :], g["W2"].rearrange("(c p) n -> p c n", p=P)).then_inc(w2_in, 16)
                sp.dma_start(xin[:, :, :], g["x"].rearrange("(t p) d -> p t d", p=P)).then_inc(x_in, 16)
                out_rows = g["out"].rearrange("(i two p) d -> p i two d", two=2, p=P)
                with sp.Fori(0, NT // 2) as i:
                    for b in range(2):
                        sp.wait_ge(y_out, 2 * i + b + 1 + CREDIT)
                        sp.dma_start(out_rows[:, bass.ds(i, 1), b, :], yout[b][:, :]).then_inc(stored[b], 16)
                for b in range(2):
                    sp.wait_ge(stored[b], (NT // 2) * 16)

            @block.gpsimd
            def _(pool):
                nc.gpsimd.tensor_tensor(vecs[:, LN1_B, :], vecs[:, LN1_B, :], vecs[:, BO, :], ALU.add).then_inc(bias_ready, 1)
                pool.wait_ge(bias_ready, 1)
                for k in range(1, NTB):
                    scale_targets(nc.gpsimd, k)
                pool.wait_ge(w_hi, 1)
                nc.gpsimd.tensor_tensor(w1_lo[:, :, :], w1[:, :, :], w1_hi[:, :, :], ALU.subtract).then_inc(w1_split, 1)
                pool.wait_ge(w_hi, 2)
                nc.gpsimd.tensor_tensor(w2_lo[:, :, :], w2[:, :, :], w2_hi[:, :, :], ALU.subtract).then_inc(w2_split, 1)
                pool.wait_ge(x_in, 16)
                for k in range(NTB):
                    pool.wait_ge(h2_ready, k + 1)
                    nc.gpsimd.tensor_tensor(xin[:, bass.ds(k * TT, TT), :], xin[:, bass.ds(k * TT, TT), :], h2[:, :, :],
                                            ALU.add).then_inc(res_ready, 1)

            @block.scalar
            def _(act):
                def centre(k):
                    for t in range(TT):
                        nb = bass.ds(k * TT + t, 1)
                        r = mask_ctx[:, bass.ds(k * BLK32 + CTX_TB + t * D, D)]
                        nc.scalar.activation(r, r, ACT.Identity, bias=ht_shift[:, nb], scale=ht_rstd[:, nb]).then_inc(centred, 1)

                def context_T(k):
                    for c in range(DC):
                        act.wait_ge(tp_ready2, DC * k + c + 2)
                        if c == 0:
                            act.wait_ge(row_ready2, TT * k + 1)
                        nc.scalar.activation(cT[:, c, :], tp[c][:, :], ACT.Copy).then_inc(cT_ready, 1)

                def h2_high(k):
                    for c in range(DC):
                        act.wait_ge(tp_ready2, DC * (NTB + k) + c + 2)
                        if k > 0 and c == 0:
                            act.wait_ge(up_ready, FC * k)
                        nc.scalar.activation(h2_hi[:, c, :], tp[c][:, :], ACT.Copy).then_inc(h2_hi_ready, 1)

                def deviation(a, b, done):
                    act.wait_ge(var2, done)
                    cols = slice(a * TT, b * TT)
                    nc.scalar.activation(rstd[:, cols], tmp[:, 3, cols], ACT.Sqrt).then_inc(std2, 1)

                centre(0)
                context_T(0)
                for k in range(1, NTB):
                    centre(k)
                act.wait_ge(w1_in, 16)
                nc.scalar.activation(w1_hi[:, :, :], w1[:, :, :], ACT.Copy).then_inc(w_hi, 1)
                context_T(1)
                deviation(0, 1, 1)
                act.wait_ge(w2_in, 16)
                nc.scalar.activation(w2_hi[:, :, :], w2[:, :, :], ACT.Copy).then_inc(w_hi, 1)
                for k in range(2, NTB):
                    context_T(k)
                h2_high(0)
                deviation(1, NTB, 2)

                for k in range(NTB):
                    for f in range(FC):
                        j = FC * k + f
                        act.wait_ge(up_ready, j + 1)
                        if j >= 2:
                            act.wait_ge(g_lo_ready, j - 1)
                        nc.scalar.activation(gelu[:, f % 2, :], up[f % 2][:, :], ACT.Gelu_apprx_tanh).then_inc(gelu_ready, 1)
                        act.wait_ge(gelu_ready, j + 1 + CREDIT)
                        if k >= 2 and f == 0:
                            act.wait_ge(row_ready2, 1 + NT + TT * (k - 1))
                        nc.scalar.activation(g_hi[:, k % 2, f, :], gelu[:, f % 2, :], ACT.Copy).then_inc(g_hi_ready, 1)
                    if k + 1 < NTB:
                        h2_high(k + 1)

            @block.vector
            def _(dve):
                chain = [0]

                def link(ins):
                    chain[0] += 1
                    ins.then_inc(link_s, 1)
                    dve.wait_ge(link_s, chain[0])

                def add_rows(k):
                    dve.wait_ge(ht_ready[k], 1)
                    for t in range(TT):
                        n = k * TT + t
                        r = mask_ctx[:, bass.ds(k * BLK32 + CTX_TB + t * D, D)]
                        dve.wait_ge(row_ready2, n + 2)
                        nc.vector.tensor_tensor(r, row[t % 2][:, :], r, ALU.add).then_inc(row_read, 1)
                        dve.wait_ge(row_read, n + 1 + CREDIT)
                        nc.vector.bn_stats(stats[:, bass.ds(n, 1), :], r).then_inc(stat2, 1)

                def spread(a, b):
                    cols = slice(a * TT, b * TT)
                    dve.wait_ge(stat2, b * TT)
                    me, qe, mo, qo = (stats[:, cols, i] for i in (1, 2, 4, 5))
                    t0, t1, t2, t3 = (tmp[:, i, cols] for i in range(4))
                    link(nc.vector.tensor_tensor(t0, me, mo, ALU.subtract))
                    link(nc.vector.tensor_tensor(t1, qe, qo, ALU.add))
                    link(nc.vector.tensor_tensor(t2, me, mo, ALU.add))
                    link(nc.vector.tensor_scalar(mean[:, cols], t2, 0.5, None, ALU.mult))
                    link(nc.vector.tensor_tensor(t0, t0, t0, ALU.mult))
                    link(nc.vector.scalar_tensor_tensor(out=t1, in0=t0, scalar=D / 4.0, in1=t1, op0=ALU.mult, op1=ALU.add))
                    nc.vector.tensor_scalar(t3, t1, 1.0 / D, EPS, ALU.mult, ALU.add).then_inc(var2, 1)

                def invert(a, b, done):
                    cols = slice(a * TT, b * TT)
                    dve.wait_ge(std2, done)
                    link(nc.vector.reciprocal(rstd[:, cols], rstd[:, cols]))
                    link(nc.vector.tensor_tensor(rstd[:, cols], rstd[:, cols], node_f[:, cols], ALU.mult))

                def second_norm(k):
                    r = res(k)
                    for t in range(TT):
                        n = k * TT + t
                        last = nc.vector.tensor_scalar(r[:, t, :], r[:, t, :], mean[:, n:n + 1], rstd[:, n:n + 1],
                                                       ALU.subtract, ALU.mult)
                        if t == TT // 2 - 1:
                            yield
                    link(last)
                    yield
                    link(nc.vector.tensor_tensor(r, r, vecs[:, LN2_G, :].unsqueeze(1).to_broadcast([P, TT, D]), ALU.mult))
                    yield
                    if k > 0:
                        dve.wait_ge(tp_ready2, 1 + DC * (k + NTB))
                        dve.wait_ge(res_ready, k)
                    for t in range(TT):
                        n = k * TT + t
                        last = nc.vector.scalar_tensor_tensor(out=h2[:, t, :], in0=vecs[:, LN2_B, :], scalar=node_f[:, n:n + 1],
                                                              in1=r[:, t, :], op0=ALU.mult, op1=ALU.add)
                        if t == TT // 2 - 1:
                            yield
                    last.then_inc(h2_ready, 1)
                    yield

                def h2_low(k):
                    for c in range(DC):
                        dve.wait_ge(h2_hi_ready, DC * k + c + 1)
                        nc.vector.tensor_tensor(h2_lo[:, c, :], tp[c][:, :], h2_hi[:, c, :], ALU.subtract).then_inc(h2_lo_ready, 1)

                def store_rows(k):
                    dve.wait_ge(res_ready, k + 1)
                    for t in range(TT):
                        b, n = t % 2, k * TT + t
                        i = n // 2
                        dve.wait_ge(row_ready2, NT + n + 2)
                        if i > 0:
                            dve.wait_ge(stored[b], 16 * i)
                        nc.vector.tensor_tensor(yout[b][:, :], row[b][:, :], xin[:, n, :], ALU.add).then_inc(y_out, 1)

                dve.wait_ge(bias_ready, 1)
                scale_targets(nc.vector, 0)
                add_rows(0)
                spread(0, 1)
                last_raw = raw_context(mask_ctx, NTB - 1)
                link(nc.vector.reciprocal(rden[:, NTB - 1, :], last_raw[:, :, VW - 1]))
                link(nc.vector.tensor_tensor(csum[:, :, :], last_raw[:, :, 0:HD], last_raw[:, :, HD:2 * HD], ALU.add))
                nc.vector.tensor_tensor(cnorm[:, :, :].rearrange("p t (h d) -> p (t h) d", h=H), csum[:, :, :],
                                        rden[:, NTB - 1, :].unsqueeze(2).to_broadcast([P, TT * H, HD]), ALU.mult).then_inc(cn_ready, 1)
                add_rows(1)
                invert(0, 1, 1)
                for _ in second_norm(0):
                    pass
                add_rows(2)
                h2_low(0)
                add_rows(NTB - 1)
                spread(1, NTB)
                invert(1, NTB, 2)
                for k in range(NTB):
                    norm = second_norm(k + 1) if k + 1 < NTB else iter(())
                    for f in range(FC):
                        dve.wait_ge(g_hi_ready, FC * k + f + 1)
                        nc.vector.tensor_tensor(g_lo[:, k % 2, f, :], gelu[:, f % 2, :], g_hi[:, k % 2, f, :],
                                                ALU.subtract).then_inc(g_lo_ready, 1)
                        next(norm, None)
                    if k + 1 < NTB:
                        h2_low(k + 1)
                    if k > 0:
                        store_rows(k - 1)
                store_rows(NTB - 1)

            @block.tensor
            def _(pe):
                for s in (row_read, y_out, gelu_ready):
                    pe.sem_inc(s, CREDIT)
                for s in (tp_ready2, row_ready2):
                    pe.sem_inc(s, 1)

                def turn(tile):
                    for c in range(DC):
                        for t in range(TT):
                            last = nc.tensor.transpose(tp[c][:, t * P:(t + 1) * P], tile(t, c), ident32[:, :])
                        last.then_inc(tp_ready2, 1)

                def turn_context(k):
                    if k == NTB - 1:
                        pe.wait_ge(cn_ready, 1)
                    if k > 0:
                        pe.wait_ge(cT_ready, DC * k)
                    c_rows = cnorm if k == NTB - 1 else normed_context(mask_ctx, k)
                    turn(lambda t, c: c_rows[:, t, c * P:(c + 1) * P])

                def project(k):
                    pe.wait_ge(cT_ready, DC * (k + 1))
                    for t in range(TT):
                        pe.wait_ge(row_read, k * TT + t + 1)
                        for c in range(DC):
                            last = nc.tensor.matmul(row[t % 2][:, :], cT[:, c, t * P:(t + 1) * P], wo[:, c, :],
                                                    start=(c == 0), stop=(c == DC - 1))
                        last.then_inc(row_ready2, 1)

                def turn_block(k):
                    pe.wait_ge(h2_ready, k + 1)
                    if k > 0:
                        pe.wait_ge(h2_lo_ready, DC * k)
                    else:
                        pe.wait_ge(cT_ready, DC * NTB)
                    turn(lambda t, c: h2[:, t, c * P:(c + 1) * P])

                turn_context(0)
                for k in range(NTB - 1):
                    project(k)
                    turn_context(k + 1)
                turn_block(0)
                project(NTB - 1)
                pe.wait_ge(row_read, NT + CREDIT)

                def up_products(k):
                    pe.wait_ge(h2_lo_ready, DC * (k + 1))
                    if k == 0:
                        pe.wait_ge(w1_split, 1)
                    for f in range(FC):
                        pe.wait_ge(gelu_ready, FC * k + f + 1)
                        terms = [(w, h, c) for c in range(DC) for w, h in ((w1_hi, h2_hi), (w1_lo, h2_hi), (w1_hi, h2_lo))]
                        for i, (w, h, c) in enumerate(terms):
                            last = nc.tensor.matmul(up[f % 2][:, :], w[:, c, f * P:(f + 1) * P], h[:, c, :],
                                                    start=(i == 0), stop=(i == len(terms) - 1))
                        last.then_inc(up_ready, 1)

                def down_products(k):
                    pe.wait_ge(g_lo_ready, FC * (k + 1))
                    if k == 0:
                        pe.wait_ge(w2_split, 1)
                    for t in range(TT):
                        pe.wait_ge(y_out, k * TT + t + 1)
                        cols = slice(t * P, (t + 1) * P)
                        terms = [(a, w, f) for f in range(FC) for a, w in ((g_hi, w2_hi), (g_hi, w2_lo), (g_lo, w2_hi))]
                        for i, (a, w, f) in enumerate(terms):
                            last = nc.tensor.matmul(row[t % 2][:, :], a[:, k % 2, f, cols], w[:, f, :],
                                                    start=(i == 0), stop=(i == len(terms) - 1))
                        last.then_inc(row_ready2, 1)

                for k in range(NTB):
                    up_products(k)
                    if k + 1 < NTB:
                        turn_block(k + 1)
                    if k > 0:
                        down_products(k - 1)
                down_products(NTB - 1)


_INS = ["x", "adj", "nodemask", "L0_gnn_h_target", "L0_gnn_ln1_scale", "L0_gnn_ln1_bias", "L0_gnn_Wq", "L0_gnn_bq",
        "L0_gnn_Wk", "L0_gnn_bk", "L0_gnn_Wv", "L0_gnn_bv", "L0_gnn_Wo", "L0_gnn_bo", "L0_gnn_ln2_scale",
        "L0_gnn_ln2_bias", "L0_gnn_W1", "L0_gnn_W2"]


def kernel(**inputs):
    import numpy as np
    import concourse.bacc as bacc
    from concourse import mybir as mb
    from concourse.bass_utils import run_bass_kernel_spmd

    nc = bacc.Bacc("TRN2", target_bir_lowering=False, num_devices=1)
    arrays, args = {}, []
    for name in _INS:
        a = np.ascontiguousarray(inputs[name])
        arrays[f"in_{name}"] = a
        args.append(nc.dram_tensor(f"in_{name}", a.shape, mb.dt.from_np(a.dtype), kind="ExternalInput").ap())
    out = nc.dram_tensor("out_y", (N, D), mb.dt.from_np(np.dtype("float32")), kind="ExternalOutput").ap()
    gnn_kernel(nc, *args, out)
    r = run_bass_kernel_spmd(nc, [arrays], core_ids=[0])
    return r.results[0]["out_y"]
```
